# Optimizing a Trainium2 kernel written in Bass

```python
import numpy as np
import jax
import jax.numpy as jnp

def _softmax(x, axis=-1):
    return jax.nn.softmax(x, axis=axis)

def _gelu(x):
    return jax.nn.gelu(x, approximate=True)

def _silu(x):
    return jax.nn.silu(x)

def _sigmoid(x):
    return jax.nn.sigmoid(x)

def _layernorm(x, axis=-1, eps=1e-05):
    m = jnp.mean(x, axis=axis, keepdims=True)
    v = jnp.var(x, axis=axis, keepdims=True)
    return (x - m) / jnp.sqrt(v + eps)

def _scatter_add(tgt, idx, src, axis=0):
    return tgt.at[idx].add(src)

def _segment_sum(src, seg, n):
    return jax.ops.segment_sum(src, seg, n)
kernel_name = 'mk_seq_postln_d1_jaxref_r8_70a0e4'

def setup_inputs(seed: int=0):
    np.random.seed(seed)
    _w = jnp.asarray

    def _L0_attn_setup():
        import jax, jax.numpy as jnp
        import numpy as np
        B, S, D_MODEL = (2, 256, 128)
        NUM_HEADS, ATTN_DIM = (16, 64)
        key = jax.random.key(seed)
        ks = jax.random.split(key, 9)
        scale = 1.0 / np.sqrt(D_MODEL)
        states = jax.random.normal(ks[0], (B, S, D_MODEL), dtype=jnp.float32)
        Wq = jax.random.normal(ks[1], (D_MODEL, NUM_HEADS * ATTN_DIM), dtype=jnp.float32) * scale
        bq = jnp.zeros((NUM_HEADS * ATTN_DIM,), dtype=jnp.float32)
        Wk = jax.random.normal(ks[2], (D_MODEL, NUM_HEADS * ATTN_DIM), dtype=jnp.float32) * scale
        bk = jnp.zeros((NUM_HEADS * ATTN_DIM,), dtype=jnp.float32)
        Wv = jax.random.normal(ks[3], (D_MODEL, NUM_HEADS * ATTN_DIM), dtype=jnp.float32) * scale
        bv = jnp.zeros((NUM_HEADS * ATTN_DIM,), dtype=jnp.float32)
        Wo = jax.random.normal(ks[4], (NUM_HEADS * ATTN_DIM, D_MODEL), dtype=jnp.float32) * scale
        bo = jnp.zeros((D_MODEL,), dtype=jnp.float32)
        return {'states': states, 'Wq': Wq, 'bq': bq, 'Wk': Wk, 'bk': bk, 'Wv': Wv, 'bv': bv, 'Wo': Wo, 'bo': bo}
    _L0_attn_in = _L0_attn_setup()

    def _L0_ffn_setup():
        import jax, jax.numpy as jnp
        import numpy as np
        E, D, F = (8, 128, 512)
        B, S = (4, 256)

        def _layernorm(x, g, b, eps=1e-05):
            mu = jnp.mean(x, axis=-1, keepdims=True)
            var = jnp.var(x, axis=-1, keepdims=True)
            return (x - mu) * jax.lax.rsqrt(var + eps) * g + b
        key = jax.random.key(seed)
        ks = jax.random.split(key, 5)
        return {'input_features': jax.random.normal(ks[0], (B, S, D), jnp.float32), 'centroids': jax.random.normal(ks[1], (E, D), jnp.float32) * 0.1, 'ln_g': jnp.ones((E, D), jnp.float32), 'ln_b': jnp.zeros((E, D), jnp.float32), 'w1': jax.random.normal(ks[2], (E, F, D), jnp.float32) * (1.0 / np.sqrt(D).astype(np.float32)), 'b1': jnp.zeros((E, F), jnp.float32), 'w2': jax.random.normal(ks[3], (E, D, F), jnp.float32) * (1.0 / np.sqrt(F).astype(np.float32)), 'b2': jnp.zeros((E, D), jnp.float32)}
    _L0_ffn_in = _L0_ffn_setup()
    _d = {'L0_attn_states': _L0_attn_in['states'], 'L0_attn_Wq': _L0_attn_in['Wq'], 'L0_attn_bq': _L0_attn_in['bq'], 'L0_attn_Wk': _L0_attn_in['Wk'], 'L0_attn_bk': _L0_attn_in['bk'], 'L0_attn_Wv': _L0_attn_in['Wv'], 'L0_attn_bv': _L0_attn_in['bv'], 'L0_attn_Wo': _L0_attn_in['Wo'], 'L0_attn_bo': _L0_attn_in['bo'], 'L0_ffn_centroids': _L0_ffn_in['centroids'], 'L0_ffn_ln_g': _L0_ffn_in['ln_g'], 'L0_ffn_ln_b': _L0_ffn_in['ln_b'], 'L0_ffn_w1': _L0_ffn_in['w1'], 'L0_ffn_b1': _L0_ffn_in['b1'], 'L0_ffn_w2': _L0_ffn_in['w2'], 'L0_ffn_b2': _L0_ffn_in['b2']}
    _x0 = _d['L0_attn_states']
    _d['L0_attn_states'] = jax.random.normal(jax.random.fold_in(jax.random.key(seed), 1), (8, 256, 128), dtype=_x0.dtype)
    del _x0
    return _d

def reference(L0_attn_states, L0_attn_Wq, L0_attn_bq, L0_attn_Wk, L0_attn_bk, L0_attn_Wv, L0_attn_bv, L0_attn_Wo, L0_attn_bo, L0_ffn_centroids, L0_ffn_ln_g, L0_ffn_ln_b, L0_ffn_w1, L0_ffn_b1, L0_ffn_w2, L0_ffn_b2):

    def _L0_attn_ref(states, Wq, bq, Wk, bk, Wv, bv, Wo, bo):
        import jax, jax.numpy as jnp
        import numpy as np
        B, S, D_MODEL = (2, 256, 128)
        NUM_HEADS, ATTN_DIM = (16, 64)
        b, s, _ = states.shape
        h, d = (NUM_HEADS, ATTN_DIM)

        def proj(W, bias):
            y = jnp.tanh(states @ W + bias)
            return y.reshape(b, s, h, d).transpose(0, 2, 1, 3)
        q, k, v = (proj(Wq, bq), proj(Wk, bk), proj(Wv, bv))
        alpha = jnp.einsum('bhqd,bhkd->bhqk', q, k) / jnp.sqrt(jnp.float32(d))
        causal = jnp.tril(jnp.ones((s, s), dtype=bool))
        alpha = jnp.where(causal, alpha, jnp.finfo(jnp.float32).min)
        alpha = jax.nn.softmax(alpha, axis=-1)
        ctx = jnp.einsum('bhqk,bhkd->bhqd', alpha, v)
        ctx = ctx.transpose(0, 2, 1, 3).reshape(b, s, h * d)
        return jnp.tanh(ctx @ Wo + bo)

    def _L0_ffn_ref(input_features, centroids, ln_g, ln_b, w1, b1, w2, b2):
        import jax, jax.numpy as jnp
        import numpy as np
        E, D, F = (8, 128, 512)
        B, S = (4, 256)

        def _layernorm(x, g, b, eps=1e-05):
            mu = jnp.mean(x, axis=-1, keepdims=True)
            var = jnp.var(x, axis=-1, keepdims=True)
            return (x - mu) * jax.lax.rsqrt(var + eps) * g + b
        Bf, Sf, Df = input_features.shape
        x = input_features.reshape(-1, Df)
        aff = x @ centroids.T
        assign = jnp.argmax(aff, axis=1)
        order = jnp.argsort(assign)
        xs = x[order]
        es = assign[order]
        alpha = jax.nn.sigmoid(jnp.take_along_axis(aff[order], es[:, None], axis=1))
        nE = centroids.shape[0]
        y = jnp.zeros_like(xs)
        for e in range(nE):
            h = _layernorm(xs, ln_g[e], ln_b[e])
            h = jax.nn.relu(h @ w1[e].T + b1[e])
            ye = xs + h @ w2[e].T + b2[e]
            y = y + jnp.where((es == e)[:, None], ye, 0.0)
        out_sorted = alpha * y + (1.0 - alpha) * xs
        inv = jnp.argsort(order)
        return out_sorted[inv].reshape(Bf, Sf, Df)
    x = L0_attn_states
    x = _layernorm(x + _L0_attn_ref(x, L0_attn_Wq, L0_attn_bq, L0_attn_Wk, L0_attn_bk, L0_attn_Wv, L0_attn_bv, L0_attn_Wo, L0_attn_bo), axis=-1)
    x = _layernorm(x + _L0_ffn_ref(x, L0_ffn_centroids, L0_ffn_ln_g, L0_ffn_ln_b, L0_ffn_w1, L0_ffn_b1, L0_ffn_w2, L0_ffn_b2), axis=-1)
    return x

_drawn_inputs = setup_inputs


def setup_inputs(seed=0):
    import zlib

    import numpy as np

    out = dict(_drawn_inputs(seed))
    spreads = {'L0_attn_bq': (0.0, 0.335),
     'L0_attn_bk': (0.0, 0.464),
     'L0_attn_bv': (0.0, 0.1),
     'L0_attn_bo': (0.0, 0.1),
     'L0_ffn_ln_g': (1.0, 0.2),
     'L0_ffn_ln_b': (0.0, 0.274),
     'L0_ffn_b1': (0.0, 0.282),
     'L0_ffn_b2': (0.0, 0.1)}
    factors = {}
    for name, (base, spread) in spreads.items():
        noise = np.random.default_rng([zlib.crc32(name.encode()), seed]).standard_normal(out[name].shape)
        drawn = base * np.exp(spread * noise) if base else spread * noise
        out[name] = jnp.asarray(drawn.astype(out[name].dtype))
    for name, factor in factors.items():
        out[name] = (out[name] * factor).astype(out[name].dtype)
    return out
```

```python
from contextlib import ExitStack

import concourse.bass as bass
from concourse import mybir
from concourse.alu_op_type import AluOpType as ALU

ACT = mybir.ActivationFunctionType
AX = mybir.AxisListType
F32 = mybir.dt.float32
F32R = mybir.dt.float32r
BF16 = mybir.dt.bfloat16
I32 = mybir.dt.int32
U32 = mybir.dt.uint32

P = 128
EPS = 1e-5
BLOCK_TILES = 4
BLOCK = BLOCK_TILES * P
PAD_TILES = 8
ROW = P + 4
ALPHA, TOKEN = P, P + 1
LOADS = 4


def work_plan(first):
    plan = []
    for i in range(8):
        if i == 0:
            plan.append(("xT", 0))
        if i == 3 and not first:
            plan.append(("proj", 0))
        if i >= 3 or not first:
            plan.append(("ctxT", i))
        if i == 1:
            plan += [("v", u) for u in range(4)]
        if 2 <= i <= 5:
            plan.append(("v", i + 2))
        if not first:
            plan += {4: [("attn", 0)], 5: [("x1T", 0)], 6: [("aff", 0)], 7: [("rank", 0)]}.get(i, [])
        plan += [("q", i), ("k", i)]
    return plan


TAIL_PLAN = [("ctxT", 0), ("ctxT", 1), ("ctxT", 2), ("proj", 0), ("attn", 0), ("x1T", 0), ("aff", 0),
             ("rank", 0), ("count", 0)]


def attention_moe(nc, x, Wq, bq, Wk, bk, Wv, bv, Wo, bo, cen, ln_g, ln_b, w1, b1, w2, b2, out):
    B, S, D = x.shape
    HD = Wq.shape[1]
    E, F, _ = w1.shape
    N = B * S
    DH = 64
    C = HD // P
    BLOCKS = N // BLOCK
    FK = F // P
    TILES = N // P + E
    DV = DH + 1
    WBC = F + FK + 2
    SLOTS = E * N + PAD_TILES * P
    assert (S, D, DH * 2, C, BLOCK) == (2 * P, P, P, 8, 2 * S) and TILES % LOADS == 0

    slots = nc.dram_tensor("slots", [SLOTS, ROW], F32, kind="Internal").ap()
    x_rows = x.rearrange("b s d -> (b s) d")
    out_rows = out.rearrange("b s d -> (b s) d")

    with ExitStack() as ctx:
        def sb(name, shape, dt=F32):
            return ctx.enter_context(nc.sbuf_tensor(name, shape, dt))

        def sem(name):
            return ctx.enter_context(nc.semaphore(name))

        ps_scores = ctx.enter_context(nc.psum_tensor("ps_scores", [P, 4, 512], F32))
        ps_ctx = ctx.enter_context(nc.psum_tensor("ps_ctx", [P, 2, 512], F32))
        ps_work = ctx.enter_context(nc.psum_tensor("ps_work", [P, 2, 512], F32))

        ident = sb("ident", [P, P])
        seen_keys = sb("seen_keys", [P, P])
        before = sb("before", [P, P], BF16)
        ones = sb("ones", [P, P], BF16)
        ones_rows = sb("ones_rows", [64, P], F32R)
        region = sb("region", [P, E])
        expert_ids = sb("expert_ids", [P, E])
        thresholds = sb("thresholds", [P, 16])
        upto = sb("upto", [P, E, E])
        tile_ids = sb("tile_ids", [P, TILES])
        fill = sb("fill", [P, ROW])
        small_rows = sb("small_rows", [P, P])
        small = sb("small", [P, P])
        bv_parts = sb("bv_parts", [64, HD], F32R)
        b2_all = sb("b2_all", [P, E, D])
        x_in = sb("x_in", [P, BLOCK_TILES, D])
        x_res = sb("x_res", [P, BLOCK_TILES, D])
        xT_hi = sb("xT_hi", [P, BLOCK], F32R)
        xT_lo = sb("xT_lo", [P, BLOCK], F32R)
        w_hi = [sb(f"w_hi{n}", [P, HD], F32R) for n in range(4)]
        w_lo = [sb(f"w_lo{n}", [P, HD], F32R) for n in range(4)]
        qT = sb("qT", [P, 2, BLOCK])
        kT = sb("kT", [P, 2, BLOCK])
        vals = sb("vals", [P, BLOCK_TILES, 2 * C, DV])
        probs = sb("probs", [P, 2, 3 * BLOCK])
        rden = sb("rden", [P, 2, BLOCK_TILES, 1])
        ctxn = sb("ctxn", [P, 2, BLOCK_TILES, 2, DH])
        cT_hi = sb("cT_hi", [P, C, BLOCK], F32R)
        cT_lo = sb("cT_lo", [P, C, BLOCK], F32R)
        aT = sb("aT", [P, BLOCK])
        bv_row = probs[0:1, 0, 0:HD]
        y = sb("y", [P, BLOCK_TILES, D])
        stats = sb("stats", [P, BLOCK_TILES, 6])
        mv = sb("mv", [P, BLOCK_TILES, 2])
        var_eps = sb("var_eps", [P, BLOCK_TILES, 1])
        minus_half = sb("minus_half", [P, BLOCK_TILES, 1])
        rstd = sb("rstd", [P, BLOCK_TILES, 1])
        pay = sb("pay", [P, BLOCK_TILES, ROW])
        x1T = sb("x1T", [P, BLOCK])
        cenT = sb("cenT", [P, E])
        aff = sb("aff", [P, BLOCK_TILES, E])
        top = sb("top", [P, BLOCK_TILES, 8])
        top_at = sb("top_at", [P, BLOCK_TILES, 8], U32)
        top_f = sb("top_f", [P, BLOCK_TILES, 1])
        exp_neg = sb("exp_neg", [P, BLOCK_TILES, 1])
        exp_one = sb("exp_one", [P, BLOCK_TILES, 1])
        chosen = sb("chosen", [P, BLOCK_TILES, E], BF16)
        seen = sb("seen", [P, BLOCK_TILES + 1, E], BF16)
        slot8 = sb("slot8", [P, BLOCK_TILES, E])
        slot8c = sb("slot8c", [P, BLOCK_TILES, E])
        slot_f = sb("slot_f", [P, BLOCK_TILES, 1])
        slot_i = sb("slot_i", [P, BLOCK_TILES], U32)
        token_f = sb("token_f", [P, BLOCK_TILES, 1])
        w1n = sb("w1n", [P, E * FK, D])
        w2n = sb("w2n", [P, E, F])
        wb = sb("wb", [P, E * WBC])
        w2T = sb("w2T", [P, E * F])
        stage = wb[:, 0:4 * HD]
        n_e = sb("n_e", [P, E])
        over = sb("over", [P, E, 16])
        tiles_e = sb("tiles_e", [P, E])
        ends8 = sb("ends8", [P, E, E])
        ends = sb("ends", [P, E])
        past = sb("past", [P, TILES, E])
        past_t = sb("past_t", [P, TILES, E])
        exp_of = sb("exp_of", [P, TILES])
        skipped = sb("skipped", [P, TILES])
        row_of = sb("row_of", [P, TILES])
        row_of2 = sb("row_of2", [P, TILES])
        table = sb("table", [P, 2, TILES], I32)
        xg = sb("xg", [P, LOADS, ROW])
        wst = sb("wst", [P, 2, WBC])
        st2 = sb("st2", [P, 2, 6])
        mv2 = sb("mv2", [P, 2, 2])
        xx = x_in
        sd2 = sb("sd2", [P, 2, 1])
        sd3 = sb("sd3", [P, 2, 1])
        rs2 = sb("rs2", [P, 2, 1])
        eps = sb("eps", [P, 1])
        hT = qT
        nrm, hin, fy, fz = (kT[:, n // 2, (n % 2) * 2 * D:(n % 2 + 1) * 2 * D].rearrange("p (a d) -> p a d", a=2)
                            for n in range(4))
        st3 = sb("st3", [P, 2, 6])
        mv3 = sb("mv3", [P, 2, 2])
        rs3 = sb("rs3", [P, 2, 1])
        fin = aT[:, 0:2 * D].rearrange("p (a d) -> p a d", a=2)

        consts_ready = sem("consts_ready")
        memset_done = sem("memset_done")
        x_loaded = sem("x_loaded")
        xres_loaded = sem("xres_loaded")
        wproj_loaded = sem("wproj_loaded")
        small_loaded = sem("small_loaded")
        wffn_loaded = sem("wffn_loaded")
        small_turned = sem("small_turned")
        small_ready = sem("small_ready")
        slots_filled = sem("slots_filled")
        wproj_split = sem("wproj_split")
        pool_step = sem("pool_step")
        dve_step = sem("dve_step")
        work_filled = [sem(f"work_filled{b}") for b in range(2)]
        work_drained = [sem(f"work_drained{b}") for b in range(2)]
        scores_ready = sem("scores_ready")
        exp_done = sem("exp_done")
        probs_ready = sem("probs_ready")
        ctx_ready = sem("ctx_ready")
        ctx_normed = sem("ctx_normed")
        y_ready = sem("y_ready")
        var_ready = sem("var_ready")
        rstd_ready = sem("rstd_ready")
        mvin_ready = sem("mvin_ready")
        mvout_ready = sem("mvout_ready")
        sdin_ready = sem("sdin_ready")
        sdout_ready = sem("sdout_ready")
        x1_ready = sem("x1_ready")
        x1T_ready = sem("x1T_ready")
        top_ready = sem("top_ready")
        expneg_ready = sem("expneg_ready")
        chosen_ready = sem("chosen_ready")
        slot_ready = sem("slot_ready")
        scatter_begun = sem("scatter_begun")
        scattered = sem("scattered")
        turned = sem("turned")
        turn_drained = sem("turn_drained")
        table_ready = sem("table_ready")
        slots_loaded = [sem(f"slots_loaded{n}") for n in range(LOADS)]
        wst_ready = sem("wst_ready")
        nrm_ready = sem("nrm_ready")
        twice_ready = sem("twice_ready")
        nT_filled = sem("nT_filled")
        hin_ready = sem("hin_ready")
        h_filled = sem("h_filled")
        hT_ready = sem("hT_ready")
        f_filled = sem("f_filled")
        f_drained = sem("f_drained")
        fin_ready = sem("fin_ready")
        stored = [sem(f"stored{n}") for n in range(LOADS)]

        first_plan, steady_plan = work_plan(True), work_plan(False)
        assert len(first_plan) % 2 == 0 and len(steady_plan) % 2 == 0

        def work(s, kind, i=0):
            if isinstance(s, str):
                plan, base = TAIL_PLAN, (len(first_plan) + (BLOCKS - 1) * len(steady_plan)) // 2
            elif isinstance(s, int) and s == 0:
                plan, base = first_plan, 0
            else:
                plan, base = steady_plan, (s - 1) * (len(steady_plan) // 2) + len(first_plan) // 2
            k = plan.index((kind, i))
            return k % 2, base + (k // 2 + 1)

        def wait(eng, s, value):
            if isinstance(value, int) and value <= 0:
                return
            eng.wait_ge(s, value)

        BQ, BK, BO, B1, LG, LB, CEN = 0, C, 2 * C, 2 * C + 1, 2 * C + 1 + E * FK, 2 * C + 1 + E * FK + E, 2 * C + 1 + E * FK + 2 * E
        SMALL = CEN + E
        N_SMALL = 7

        block = ctx.enter_context(nc.Block())

        @block.sync
        def _(sp):
            def x_tiles(s):
                return x_rows[bass.ds(s * BLOCK, BLOCK), :].rearrange("(t p) d -> p t d", p=P)

            sp.dma_start(x_in[:], x_tiles(0)).then_inc(x_loaded, 16)
            for n, w in enumerate((Wq, Wk, Wv)):
                sp.dma_start(stage[:, n * HD:(n + 1) * HD], w).then_inc(wproj_loaded, 16)
            sp.dma_start(stage[:, 3 * HD:4 * HD].rearrange("p (c d) -> p c d", c=C),
                         Wo.rearrange("(c p) d -> p c d", p=P)).then_inc(wproj_loaded, 16)
            sp.dma_start(w1n[:].rearrange("p (e k) d -> p e k d", e=E),
                         w1.rearrange("e (k p) d -> p e k d", p=P)).then_inc(wffn_loaded, 16)
            sp.dma_start(w2n[:], w2.rearrange("e d f -> d e f")).then_inc(wffn_loaded, 16)
            sp.dma_start(b2_all[:].rearrange("p e d -> p (e d)"),
                         b2.rearrange("e d -> (e d)").partition_broadcast(P)).then_inc(wffn_loaded, 16)
            sp.wait_ge(consts_ready, 1)
            tiles = SLOTS // P
            per = tiles // 4
            view = slots.rearrange("(n p) c -> p n c", p=P)
            for n in range(4):
                sp.dma_start(view[:, n * per:(n + 1) * per, :],
                             fill[:].unsqueeze(1).broadcast_to([P, per, ROW])).then_inc(slots_filled, 16)

            def body(s):
                b, n = work(s - 1, "xT")
                sp.wait_ge(work_drained[b], n)
                sp.dma_start(x_in[:], x_tiles(s)).then_inc(x_loaded, 16)
                wait(sp, y_ready, s - 1)
                sp.dma_start(x_res[:], x_tiles(s - 1)).then_inc(xres_loaded, 16)

            body(1)
            with sp.Fori(2, BLOCKS) as s:
                body(s)
            sp.wait_ge(y_ready, BLOCKS - 1)
            sp.dma_start(x_res[:], x_tiles(BLOCKS - 1)).then_inc(xres_loaded, 16)

            sp.wait_ge(table_ready, 1)
            sp.wait_ge(scattered, 16 * BLOCKS * BLOCK_TILES)
            for j in range(TILES):
                row = sp.value_load(table[0:1, 1, j:j + 1], min_val=0, max_val=SLOTS - P)
                if j >= LOADS:
                    sp.wait_ge(stored[j % LOADS], 16 * (j // LOADS))
                sp.dma_start(xg[:, j % LOADS, :], slots[bass.ds(row, P), :]).then_inc(slots_loaded[j % LOADS], 16)

        @block.gpsimd
        def _(pool):
            count = [0]

            def link(ins):
                count[0] += 1
                ins.then_inc(pool_step, 1)
                pool.wait_ge(pool_step, count[0])

            link(pool.memset(fill[:], 0.0))
            link(pool.iota(fill[:].bitcast(I32)[:, TOKEN:TOKEN + 1], pattern=[[0, 1]], base=N, channel_multiplier=1))
            pool.nop().then_inc(consts_ready, 1)
            pool.memset(small_rows[:], 0.0).then_inc(memset_done, 1)
            link(pool.memset(ident[:], 0.0))
            link(pool.affine_select(out=ident[:], in_=ident[:], compare_op=ALU.not_equal, fill=1.0, base=0,
                                    pattern=[[-1, P]], channel_multiplier=1))
            pool.wait_ge(memset_done, 1)
            for row, n, src in ((BQ, C, bq.rearrange("(c p) -> c p", p=P)), (BK, C, bk.rearrange("(c p) -> c p", p=P)),
                                (BO, 1, bo.rearrange("(c p) -> c p", p=P)), (B1, E * FK, b1.rearrange("e (k p) -> (e k) p", p=P)),
                                (LG, E, ln_g), (LB, E, ln_b), (CEN, E, cen)):
                pool.dma_start(small_rows[row:row + n, :], src).then_inc(small_loaded, 16)
            pool.dma_start(bv_row, bv.rearrange("(o n) -> o n", o=1)).then_inc(small_loaded, 16)
            link(pool.memset(ones[:], 1.0))
            link(pool.affine_select(out=before[:], in_=ones[:], compare_op=ALU.is_gt, fill=0.0, base=0,
                                    pattern=[[1, P]], channel_multiplier=-1))
            link(pool.memset(seen_keys[:], 1.0))
            link(pool.affine_select(out=seen_keys[:], in_=seen_keys[:], compare_op=ALU.is_ge, fill=0.0, base=0,
                                    pattern=[[1, P]], channel_multiplier=-1))
            pool.iota(region[:], pattern=[[N, E]], base=0, channel_multiplier=0, allow_small_or_imprecise_dtypes=True)
            pool.iota(expert_ids[:], pattern=[[1, E]], base=0, channel_multiplier=0, allow_small_or_imprecise_dtypes=True)
            pool.iota(thresholds[:], pattern=[[P, 16]], base=0, channel_multiplier=0, allow_small_or_imprecise_dtypes=True)
            pool.iota(tile_ids[:], pattern=[[1, TILES]], base=0, channel_multiplier=0, allow_small_or_imprecise_dtypes=True)
            pool.iota(token_f[:], pattern=[[P, BLOCK_TILES]], base=0, channel_multiplier=1, allow_small_or_imprecise_dtypes=True)
            link(pool.memset(upto[:], 1.0))
            link(pool.affine_select(out=upto[:], in_=upto[:], compare_op=ALU.is_ge, fill=0.0, base=0,
                                    pattern=[[1, E], [-1, E]], channel_multiplier=0))
            link(pool.memset(vals[:, :, :, DH:DV], 1.0))
            link(pool.memset(pay[:], 0.0))
            link(pool.memset(minus_half[:], -0.5))
            link(pool.memset(eps[:], EPS))
            link(pool.memset(bv_parts[:].bitcast(F32), 0.0))
            link(pool.memset(ones_rows[:].bitcast(F32), 1.0))
            pool.nop().then_inc(consts_ready, 1)
            pool.wait_ge(wproj_loaded, 64)
            for n in (2, 3):
                src = stage[:, n * HD:(n + 1) * HD]
                link(pool.tensor_copy(w_hi[n][:], src))
                pool.tensor_tensor(w_lo[n][:], src, w_hi[n][:], ALU.subtract).then_inc(wproj_split, 1)

            def mask(g, par):
                for part, (start, end, step) in enumerate(((0, 2 * BLOCK, S), (2 * BLOCK, 3 * BLOCK, P))):
                    pool.wait_ge(exp_done, 2 * g + part + 1)
                    v = probs[:, par, start:end].rearrange("p (n q) -> p n q", q=step)[:, :, 0:P]
                    pool.tensor_tensor(v, v, seen_keys[:].unsqueeze(1).broadcast_to([P, 4, P]),
                                       ALU.mult).then_inc(probs_ready, 1)

            def root(b):
                pool.wait_ge(var_ready, b + 1)
                pool.tensor_tensor(rstd[:], var_eps[:], minus_half[:], ALU.pow).then_inc(rstd_ready, 1)

            def scatter(b):
                pool.wait_ge(slot_ready, b + 1)
                pool.sem_inc(scatter_begun, 1)
                for t in range(BLOCK_TILES):
                    pool.indirect_dma_start(slots, bass.IndirectOffsetOnAxis(ap=slot_i[:, t:t + 1], axis=0),
                                            pay[:, t, :], None, bounds_check=SLOTS - 1,
                                            oob_is_err=False).then_inc(scattered, 16)

            def body(s, first=False):
                for i in range(8):
                    if i or not first:
                        mask(8 * s - 1 + i, (i + 1) % 2)
                    if i == 4 and not first:
                        root(s - 1)
                if not first:
                    scatter(s - 1)

            body(0, True)
            pool.wait_ge(slots_filled, 64)
            with pool.Fori(1, BLOCKS) as s:
                body(s)
            mask(8 * BLOCKS - 1, 1)
            root(BLOCKS - 1)
            scatter(BLOCKS - 1)

            pool.wait_ge(table_ready, 1)
            pool.wait_ge(turn_drained, 2 * E)

            def store(j):
                pool.wait_ge(fin_ready, j + 1)
                pool.indirect_dma_start(out_rows, bass.IndirectOffsetOnAxis(
                    ap=xg[:].bitcast(U32)[:, j % LOADS, TOKEN:TOKEN + 1], axis=0), fin[:, j % 2, :], None,
                    bounds_check=N - 1, oob_is_err=False).then_inc(stored[j % LOADS], 16)

            for j in range(TILES + 2):
                if j < TILES:
                    if j >= 2:
                        pool.wait_ge(hT_ready, FK * (j - 1))
                    e = pool.value_load(table[0:1, 0, j:j + 1], min_val=0, max_val=E - 1)
                    pool.tensor_copy(wst[:, j % 2, :], wb[:, bass.ds(e * WBC, WBC)]).then_inc(wst_ready, 1)
                if j >= 2:
                    store(j - 2)
            for q in range(LOADS):
                pool.wait_ge(stored[q], 16 * (TILES // LOADS))

        @block.scalar
        def _(act):
            def tanh_qk(s, i):
                par = i % 2
                for kind, dst, base in (("q", qT, BQ), ("k", kT, BK)):
                    b, n = work(s, kind, i)
                    act.wait_ge(work_filled[b], n)
                    act.activation(dst[:, par, :], ps_work[:, b, :], ACT.Tanh,
                                   bias=small[:, base + i:base + i + 1]).then_inc(work_drained[b], 1)

            def tanh_v(s, u):
                b, n = work(s, "v", u)
                act.wait_ge(work_filled[b], n)
                t, half = u % 4, u // 4
                act.activation(vals[:, t, half * C:(half + 1) * C, 0:DH],
                               ps_work[:, b, :].rearrange("p (h d) -> p h d", d=DH), ACT.Tanh).then_inc(work_drained[b], 1)

            def exp_scores(g, par):
                act.wait_ge(scores_ready, g + 1)
                ps = ps_scores[:].rearrange("p (h z) c -> p h z c", h=2)
                act.activation(probs[:, par, 0:2 * BLOCK].rearrange("p (h c) -> p h c", h=2), ps[:, :, 0, :],
                               ACT.Exp, scale=DH ** -0.5).then_inc(exp_done, 1)
                act.activation(probs[:, par, 2 * BLOCK:3 * BLOCK].rearrange("p (h c) -> p h c", h=2),
                               ps[:, :, 1, 0:S], ACT.Exp, scale=DH ** -0.5).then_inc(exp_done, 1)

            def tanh_out(s):
                b, n = work(s, "proj")
                act.wait_ge(work_filled[b], n)
                act.activation(aT[:], ps_work[:, b, :], ACT.Tanh, bias=small[:, BO:BO + 1]).then_inc(work_drained[b], 1)

            def copy_x1T(s):
                b, n = work(s, "x1T")
                act.wait_ge(work_filled[b], n)
                act.copy(x1T[:], ps_work[:, b, :]).then_inc(work_drained[b], 1)

            def exp_gate(blk):
                act.wait_ge(top_ready, blk + 1)
                act.activation(exp_neg[:], top[:, :, 0:1], ACT.Exp, scale=-1.0).then_inc(expneg_ready, 1)

            def body(s, first=False):
                for i in range(8):
                    if i or not first:
                        exp_scores(8 * s - 1 + i, (i + 1) % 2)
                    if i == 3 and not first:
                        tanh_out(s)
                    if i == 1:
                        for u in range(4):
                            tanh_v(s, u)
                    if 2 <= i <= 5:
                        tanh_v(s, i + 2)
                    if i == 5 and not first:
                        copy_x1T(s)
                    if i == 7 and not first:
                        exp_gate(s - 1)
                    tanh_qk(s, i)

            act.wait_ge(small_turned, 1)
            act.copy(small[:, 0:SMALL], ps_ctx[:, 0, 0:SMALL]).then_inc(small_ready, 1)
            act.wait_ge(small_ready, 1)
            body(0, True)
            with act.Fori(1, BLOCKS) as s:
                body(s)
            exp_scores(8 * BLOCKS - 1, 1)

            wbv = wb[:].rearrange("p (e c) -> p e c", e=E)

            def drain_turned(n):
                act.wait_ge(turned, n + 1)
                dst = wbv[:, n, 0:F] if n < E else w2T[:, (n - E) * F:(n - E + 1) * F]
                act.copy(dst, ps_scores[:, n % 4, :]).then_inc(turn_drained, 1)

            for n in range(8):
                drain_turned(n)
            tanh_out("tail")
            for n in range(8, 12):
                drain_turned(n)
            copy_x1T("tail")
            for n in range(12, 16):
                drain_turned(n)
            exp_gate(BLOCKS - 1)

            def relu(j):
                act.wait_ge(h_filled, j + 1)
                for k in range(FK):
                    act.activation(hT[:, j % 2, k * P:(k + 1) * P], ps_scores[:, j % 2, k * P:(k + 1) * P], ACT.Relu,
                                   bias=wst[:, j % 2, F + k:F + k + 1]).then_inc(hT_ready, 1)

            for j in range(-1, TILES + 1):
                if j + 1 < TILES:
                    q = (j + 1) % LOADS
                    act.wait_ge(slots_loaded[q], 16 * ((j + 1) // LOADS + 1))
                    act.mul(xx[:, q, :], xg[:, q, 0:D], 2.0).then_inc(twice_ready, 1)
                    act.wait_ge(mvin_ready, j + 2)
                    act.activation(sd2[:, (j + 1) % 2, :], mv2[:, (j + 1) % 2, 1:2], ACT.Sqrt,
                                   bias=eps[:]).then_inc(sdin_ready, 1)
                if 0 <= j < TILES:
                    relu(j)
                if j >= 1:
                    act.wait_ge(mvout_ready, j)
                    act.activation(sd3[:, (j - 1) % 2, :], mv3[:, (j - 1) % 2, 1:2], ACT.Sqrt,
                                   bias=eps[:]).then_inc(sdout_ready, 1)

        @block.vector
        def _(dve):
            count = [0]

            def link(ins):
                count[0] = count[0] + 1
                ins.then_inc(dve_step, 1)
                dve.wait_ge(dve_step, count[0])

            dve.wait_ge(wproj_loaded, 64)
            for n in (0, 1):
                src = stage[:, n * HD:(n + 1) * HD]
                link(dve.tensor_copy(w_hi[n][:], src))
                dve.tensor_tensor(w_lo[n][:], src, w_hi[n][:], ALU.subtract).then_inc(wproj_split, 1)
            dve.wait_ge(small_ready, 1)
            dve.wait_ge(consts_ready, 2)
            dve.wait_ge(small_loaded, 16 * (N_SMALL + 1))
            link(dve.tensor_copy(cenT[:], small[:, CEN:CEN + E]))
            link(dve.tensor_copy(bv_parts[0:1, :], bv_row))
            dve.tensor_tensor(bv_parts[32:33, :], bv_row, bv_parts[0:1, :], ALU.subtract).then_inc(wproj_split, 1)
            link(dve.memset(seen[:, BLOCK_TILES, :], 0.0))

            def split_xT(s):
                b, n = work(s, "xT")
                dve.wait_ge(work_filled[b], n)
                link(dve.tensor_copy(xT_hi[:], ps_work[:, b, :]))
                dve.tensor_tensor(xT_lo[:], ps_work[:, b, :], xT_hi[:], ALU.subtract).then_inc(work_drained[b], 1)

            def normalise(g, par):
                dve.wait_ge(ctx_ready, g + 1)
                c = ps_ctx[:, :, 0:BLOCK_TILES * DV].rearrange("p h (t e) -> p h t e", e=DV)
                link(dve.reciprocal(rden[:], c[:, :, :, DH:DV]))
                dve.tensor_tensor(ctxn[:, par].rearrange("p t h d -> p h t d"), c[:, :, :, 0:DH],
                                  rden[:].broadcast_to([P, 2, BLOCK_TILES, DH]), ALU.mult).then_inc(ctx_normed, 1)

            def split_cT(s, i, c):
                b, n = work(s, "ctxT", i)
                dve.wait_ge(work_filled[b], n)
                link(dve.tensor_copy(cT_hi[:, c, :], ps_work[:, b, :]))
                dve.tensor_tensor(cT_lo[:, c, :], ps_work[:, b, :], cT_hi[:, c, :], ALU.subtract).then_inc(work_drained[b], 1)

            def layer_norm_1(s, blk):
                b, n = work(s, "attn")
                dve.wait_ge(work_filled[b], n)
                dve.wait_ge(xres_loaded, 16 * (blk + 1))
                dve.tensor_tensor(y[:].rearrange("p t d -> p (t d)"), ps_work[:, b, :],
                                  x_res[:].rearrange("p t d -> p (t d)"), ALU.add).then_inc(work_drained[b], 1)
                dve.wait_ge(work_drained[b], n)
                for t in range(BLOCK_TILES):
                    last = dve.bn_stats(stats[:, t, :], y[:, t, :])
                link(last)
                dve.sem_inc(y_ready, 1)
                for t in range(BLOCK_TILES):
                    last = dve.bn_aggr(mv[:, t, :], stats[:, t, :])
                link(last)
                dve.tensor_scalar(var_eps[:], mv[:, :, 1:2], EPS, None, ALU.add).then_inc(var_ready, 1)
                dve.wait_ge(rstd_ready, blk + 1)
                wait(dve, scattered, 16 * BLOCK_TILES * blk)
                for t in range(BLOCK_TILES):
                    last = dve.tensor_scalar(pay[:, t, 0:D], y[:, t, :], mv[:, t, 0:1], rstd[:, t, :],
                                             ALU.subtract, ALU.mult)
                last.then_inc(x1_ready, 1)

            def choose(s, blk):
                b, n = work(s, "aff")
                dve.wait_ge(work_filled[b], n)
                dve.tensor_copy(aff[:].rearrange("p t e -> p (t e)"),
                                ps_work[:, b, 0:BLOCK_TILES * E]).then_inc(work_drained[b], 1)
                dve.wait_ge(work_drained[b], n)
                for t in range(BLOCK_TILES):
                    last = dve.max(top[:, t, :], aff[:, t, :])
                last.then_inc(top_ready, 1)
                dve.wait_ge(top_ready, blk + 1)
                for t in range(BLOCK_TILES):
                    last = dve.max_index(top_at[:, t, :], top[:, t, :], aff[:, t, :])
                link(last)
                link(dve.tensor_copy(top_f[:], top_at[:, :, 0:1]))
                dve.tensor_copy(seen[:, 0, :], seen[:, BLOCK_TILES, :])
                link(dve.tensor_tensor(chosen[:], expert_ids[:].unsqueeze(1).broadcast_to([P, BLOCK_TILES, E]),
                                       top_f[:].broadcast_to([P, BLOCK_TILES, E]), ALU.is_equal))
                for t in range(BLOCK_TILES):
                    link(dve.tensor_tensor(seen[:, t + 1, :], seen[:, t, :], chosen[:, t, :], ALU.add))
                dve.sem_inc(chosen_ready, 1)

            def place(s, blk):
                b, n = work(s, "rank")
                dve.wait_ge(expneg_ready, blk + 1)
                link(dve.tensor_scalar(exp_one[:], exp_neg[:], 1.0, None, ALU.add))
                dve.reciprocal(pay[:, :, ALPHA:ALPHA + 1], exp_one[:])
                dve.tensor_copy(pay[:].bitcast(I32)[:, :, TOKEN:TOKEN + 1], token_f[:])
                dve.wait_ge(work_filled[b], n)
                dve.tensor_tensor(slot8[:], ps_work[:, b, 0:BLOCK_TILES * E].rearrange("p (t e) -> p t e", e=E),
                                  region[:].unsqueeze(1).broadcast_to([P, BLOCK_TILES, E]),
                                  ALU.add).then_inc(work_drained[b], 1)
                dve.wait_ge(work_drained[b], n)
                link(dve.tensor_tensor(slot8c[:], slot8[:], chosen[:], ALU.mult))
                link(dve.tensor_reduce(slot_f[:], slot8c[:], AX.X, ALU.add))
                dve.tensor_scalar(token_f[:], token_f[:], float(BLOCK), None, ALU.add)
                dve.tensor_copy(slot_i[:].unsqueeze(2), slot_f[:]).then_inc(slot_ready, 1)

            def body(s, first=False):
                for i in range(8):
                    if i == 0:
                        split_xT(s)
                    if i >= 2 or not first:
                        normalise(8 * s - 2 + i, i % 2)
                    if i >= 3 or not first:
                        split_cT(s, i, (i + 5) % 8)
                    if not first:
                        if i == 4:
                            layer_norm_1(s, s - 1)
                        if i == 6:
                            choose(s, s - 1)
                        if i == 7:
                            place(s, s - 1)

            body(0, True)
            for s in range(1, BLOCKS):
                body(s)
            normalise(8 * BLOCKS - 2, 0)
            split_cT("tail", 0, C - 3)
            normalise(8 * BLOCKS - 1, 1)
            split_cT("tail", 1, C - 2)
            split_cT("tail", 2, C - 1)
            wbv = wb[:].rearrange("p (e c) -> p e c", e=E)
            dve.tensor_copy(wbv[:, :, F:F + FK], small[:, B1:B1 + E * FK].rearrange("p (e k) -> p e k", e=E))
            dve.tensor_copy(wbv[:, :, F + FK:F + FK + 1], small[:, LG:LG + E].unsqueeze(2))
            dve.tensor_copy(wbv[:, :, F + FK + 1:F + FK + 2], small[:, LB:LB + E].unsqueeze(2))
            layer_norm_1("tail", BLOCKS - 1)
            choose("tail", BLOCKS - 1)
            place("tail", BLOCKS - 1)

            b, n = work("tail", "count")
            dve.wait_ge(work_filled[b], n)
            link(dve.tensor_copy(n_e[:], ps_work[:, b, 0:E]))
            link(dve.tensor_tensor(over[:], n_e[:].unsqueeze(2).broadcast_to([P, E, 16]),
                                   thresholds[:].unsqueeze(1).broadcast_to([P, E, 16]), ALU.is_gt))
            link(dve.tensor_reduce(tiles_e[:].unsqueeze(2), over[:], AX.X, ALU.add))
            link(dve.tensor_tensor(ends8[:], upto[:], tiles_e[:].unsqueeze(1).broadcast_to([P, E, E]), ALU.mult))
            link(dve.tensor_reduce(ends[:].unsqueeze(2), ends8[:], AX.X, ALU.add))
            link(dve.tensor_tensor(past[:], tile_ids[:].unsqueeze(2).broadcast_to([P, TILES, E]),
                                   ends[:].unsqueeze(1).broadcast_to([P, TILES, E]), ALU.is_ge))
            dve.tensor_reduce(exp_of[:].unsqueeze(2), past[:], AX.X, ALU.add)
            link(dve.tensor_tensor(past_t[:], past[:], tiles_e[:].unsqueeze(1).broadcast_to([P, TILES, E]), ALU.mult))
            link(dve.tensor_reduce(skipped[:].unsqueeze(2), past_t[:], AX.X, ALU.add))
            link(dve.tensor_tensor(row_of[:], tile_ids[:], skipped[:], ALU.subtract))
            link(dve.tensor_scalar(row_of2[:], row_of[:], float(P), None, ALU.mult))
            dve.tensor_scalar(table[:, 0, :], exp_of[:], float(E - 1), None, ALU.min)
            link(dve.scalar_tensor_tensor(out=table[:, 1, :], in0=exp_of[:], scalar=float(N), in1=row_of2[:],
                                          op0=ALU.mult, op1=ALU.add))
            dve.sem_inc(table_ready, 1)

            def norm_in(j):
                p, q = j % 2, j % LOADS
                dve.wait_ge(slots_loaded[q], 16 * (j // LOADS + 1))
                link(dve.bn_stats(st2[:, p, :], xg[:, q, 0:D]))
                dve.bn_aggr(mv2[:, p, :], st2[:, p, :]).then_inc(mvin_ready, 1)
                dve.wait_ge(sdin_ready, j + 1)
                link(dve.reciprocal(rs2[:, p, :], sd2[:, p, :]))
                dve.tensor_scalar(nrm[:, p, :], xg[:, q, 0:D], mv2[:, p, 0:1], rs2[:, p, :], ALU.subtract,
                                  ALU.mult).then_inc(nrm_ready, 1)

            def scale_in(j):
                p = j % 2
                dve.wait_ge(nT_filled, j + 1)
                dve.wait_ge(wst_ready, j + 1)
                dve.tensor_scalar(hin[:, p, :], ps_work[:, p, 0:P], wst[:, p, F + FK:F + FK + 1],
                                  wst[:, p, F + FK + 1:F + FK + 2], ALU.mult, ALU.add).then_inc(hin_ready, 1)

            def norm_out(j):
                p, q = j % 2, j % LOADS
                e = dve.value_load(table[0:1, 0, j:j + 1], min_val=0, max_val=E - 1)
                dve.wait_ge(f_filled, j + 1)
                dve.tensor_tensor(fy[:, p, :], ps_scores[:, 2 + p, 0:D],
                                  b2_all[:].rearrange("p e d -> p (e d)")[:, bass.ds(e * D, D)],
                                  ALU.add).then_inc(f_drained, 1)
                dve.wait_ge(f_drained, j + 1)
                dve.wait_ge(twice_ready, j + 1)
                link(dve.scalar_tensor_tensor(out=fz[:, p, :], in0=fy[:, p, :], scalar=xg[:, q, ALPHA:ALPHA + 1],
                                              in1=xx[:, q, :], op0=ALU.mult, op1=ALU.add))
                link(dve.bn_stats(st3[:, p, :], fz[:, p, :]))
                dve.bn_aggr(mv3[:, p, :], st3[:, p, :]).then_inc(mvout_ready, 1)
                dve.wait_ge(sdout_ready, j + 1)
                link(dve.reciprocal(rs3[:, p, :], sd3[:, p, :]))
                if j >= 2:
                    dve.wait_ge(stored[(j - 2) % LOADS], 16 * ((j - 2) // LOADS + 1))
                dve.tensor_scalar(fin[:, p, :], fz[:, p, :], mv3[:, p, 0:1], rs3[:, p, :], ALU.subtract,
                                  ALU.mult).then_inc(fin_ready, 1)

            for j in range(-1, TILES + 1):
                if j + 1 < TILES:
                    norm_in(j + 1)
                    scale_in(j + 1)
                if j >= 1:
                    norm_out(j - 1)

        @block.tensor
        def _(pe):
            def fill_work(s, kind, i=0):
                b, n = work(s, kind, i)
                wait(pe, work_drained[b], n - 1)
                return b

            def transposes(b, tiles):
                for t in range(BLOCK_TILES):
                    last = pe.transpose(ps_work[:, b, t * P:(t + 1) * P], tiles[t], ident[:])
                last.then_inc(work_filled[b], 1)

            def product3(o, lhs, rhs, start=True, stop=True):
                pe.matmul(o, lhs[0], rhs[0], start=start, stop=False)
                pe.matmul(o, lhs[0], rhs[1], start=False, stop=False)
                return pe.matmul(o, lhs[1], rhs[0], start=False, stop=stop)

            def turn_x(s):
                pe.wait_ge(x_loaded, 16 * (s + 1))
                b = fill_work(s, "xT")
                transposes(b, [x_in[:, t, :] for t in range(BLOCK_TILES)])

            def drained(s, kind, i=0):
                b, n = work(s, kind, i)
                pe.wait_ge(work_drained[b], n)

            def project_qk(s, i):
                for w, kind in enumerate(("q", "k")):
                    b = fill_work(s, kind, i)
                    if i == 0:
                        drained(s, "xT")
                    cols = slice(i * P, (i + 1) * P)
                    product3(ps_work[:, b, :], (w_hi[w][:, cols], w_lo[w][:, cols]),
                             (xT_hi[:], xT_lo[:])).then_inc(work_filled[b], 1)

            def project_v(s, u):
                b = fill_work(s, "v", u)
                t, half = u % 4, u // 4
                toks, cols = slice(t * P, (t + 1) * P), slice(half * 512, (half + 1) * 512)
                pe.matmul(ps_work[:, b, :], ones_rows[:], bv_parts[:, cols], start=True, stop=False)
                product3(ps_work[:, b, :], (xT_hi[:, toks], xT_lo[:, toks]), (w_hi[2][:, cols], w_lo[2][:, cols]),
                         start=False).then_inc(work_filled[b], 1)

            def scores(g, par, s, i):
                if isinstance(s, str):
                    for kind in "qk":
                        b, n = work(BLOCKS - 1, kind, 7)
                        pe.wait_ge(work_drained[b], n)
                elif i:
                    drained(s, "q", i - 1)
                    drained(s, "k", i - 1)
                else:
                    drained_before(s)
                wait(pe, exp_done, 2 * g)
                for hh in range(2):
                    rows = slice(hh * DH, (hh + 1) * DH)
                    for bb in range(2):
                        o = bb * S
                        pe.matmul(ps_scores[:, 2 * hh, o:o + S], kT[rows, par, o:o + P], qT[rows, par, o:o + S],
                                  start=True, stop=True)
                    for bb in range(2):
                        o = bb * S + P
                        last = pe.matmul(ps_scores[:, 2 * hh + 1, bb * P:(bb + 1) * P], kT[rows, par, o:o + P],
                                         qT[rows, par, o:o + P], start=True, stop=True)
                last.then_inc(scores_ready, 1)

            def drained_before(s):
                for kind in "qk":
                    k = steady_plan.index((kind, 7)) - len(steady_plan)
                    base = (s - 1) * (len(steady_plan) // 2) + len(first_plan) // 2
                    pe.wait_ge(work_drained[k % 2], base + (k // 2 + 1))

            def contexts(g, par, pair):
                pe.wait_ge(probs_ready, 2 * (g + 1))
                wait(pe, ctx_normed, g)
                for hh in range(2):
                    h = 2 * pair + hh
                    first = probs[:, par, hh * BLOCK:(hh + 1) * BLOCK]
                    second = probs[:, par, 2 * BLOCK + hh * S:2 * BLOCK + (hh + 1) * S]
                    for bb in range(2):
                        t0, t1 = 2 * bb, 2 * bb + 1
                        o0, o1 = ps_ctx[:, hh, t0 * DV:(t0 + 1) * DV], ps_ctx[:, hh, t1 * DV:(t1 + 1) * DV]
                        pe.matmul(o0, first[:, bb * S:bb * S + P], vals[:, t0, h, :], start=True, stop=True)
                        pe.matmul(o1, first[:, bb * S + P:bb * S + S], vals[:, t0, h, :], start=True, stop=False)
                        last = pe.matmul(o1, second[:, bb * P:(bb + 1) * P], vals[:, t1, h, :],
                                         start=False, stop=True)
                last.then_inc(ctx_ready, 1)

            def turn_ctx(s, i, g, par):
                pe.wait_ge(ctx_normed, g + 1)
                b = fill_work(s, "ctxT", i)
                transposes(b, [ctxn[:, par, t].rearrange("p h d -> p (h d)") for t in range(BLOCK_TILES)])

            def project_out(s):
                b = fill_work(s, "proj")
                if isinstance(s, str):
                    drained(s, "ctxT", 2)
                else:
                    drained(s, "ctxT", 2)
                for c in range(C):
                    cols = slice(c * P, (c + 1) * P)
                    last = product3(ps_work[:, b, :], (w_hi[3][:, cols], w_lo[3][:, cols]),
                                    (cT_hi[:, c, :], cT_lo[:, c, :]), start=(c == 0), stop=(c == C - 1))
                last.then_inc(work_filled[b], 1)

            def turn_attn(s):
                drained(s, "proj")
                b = fill_work(s, "attn")
                transposes(b, [aT[:, t * P:(t + 1) * P] for t in range(BLOCK_TILES)])

            def turn_x1(s, blk):
                pe.wait_ge(x1_ready, blk + 1)
                b = fill_work(s, "x1T")
                transposes(b, [pay[:, t, 0:D] for t in range(BLOCK_TILES)])

            def affinities(s):
                drained(s, "x1T")
                b = fill_work(s, "aff")
                for t in range(BLOCK_TILES):
                    last = pe.matmul(ps_work[:, b, t * E:(t + 1) * E], x1T[:, t * P:(t + 1) * P], cenT[:],
                                     start=True, stop=True)
                last.then_inc(work_filled[b], 1)

            def ranks(s, blk):
                pe.wait_ge(chosen_ready, blk + 1)
                b = fill_work(s, "rank")
                o = ps_work[:, b, 0:BLOCK_TILES * E]
                pe.matmul(o, before[:], chosen[:].rearrange("p t e -> p (t e)"), start=True, stop=False)
                pe.matmul(o, ones[:], seen[:, 0:BLOCK_TILES, :].rearrange("p t e -> p (t e)"), start=False,
                          stop=True).then_inc(work_filled[b], 1)

            def body(s, first=False):
                for i in range(8):
                    if i == 0:
                        turn_x(s)
                    if i or not first:
                        scores(8 * s - 1 + i, (i + 1) % 2, s, i)
                    if i >= 2 or not first:
                        if i == 2:
                            drained(s, "v", 3)
                            drained(s, "v", 2)
                        if i == 6:
                            drained(s, "v", 7)
                            drained(s, "v", 6)
                        contexts(8 * s - 2 + i, i % 2, (i - 2) % 8)
                    if i == 3 and not first:
                        project_out(s)
                    if i >= 3 or not first:
                        turn_ctx(s, i, 8 * s - 3 + i, (i + 1) % 2)
                    if i == 1:
                        for u in range(4):
                            project_v(s, u)
                    if 2 <= i <= 5:
                        project_v(s, i + 2)
                    if not first:
                        if i == 4:
                            turn_attn(s)
                        if i == 5:
                            turn_x1(s, s - 1)
                        if i == 6:
                            affinities(s)
                        if i == 7:
                            ranks(s, s - 1)
                    project_qk(s, i)

            pe.wait_ge(consts_ready, 1)
            pe.wait_ge(pool_step, 4)
            pe.wait_ge(small_loaded, 16 * (N_SMALL + 1))
            pe.transpose(ps_ctx[:, 0, 0:P], small_rows[:], ident[:]).then_inc(small_turned, 1)
            pe.wait_ge(consts_ready, 2)
            pe.wait_ge(wproj_split, 5)
            body(0, True)
            with pe.Fori(1, BLOCKS) as s:
                body(s)

            def turn_weights(n):
                pe.wait_ge(exp_done, 16 * BLOCKS)
                if n >= 4:
                    pe.wait_ge(turn_drained, n - 3)
                for k in range(FK):
                    src = w1n[:, n * FK + k, :] if n < E else w2n[:, n - E, k * P:(k + 1) * P]
                    last = pe.transpose(ps_scores[:, n % 4, k * P:(k + 1) * P], src, ident[:])
                last.then_inc(turned, 1)

            scores(8 * BLOCKS - 1, 1, "tail", 0)
            contexts(8 * BLOCKS - 2, 0, C - 2)
            turn_ctx("tail", 0, 8 * BLOCKS - 3, 1)
            pe.wait_ge(wffn_loaded, 48)
            contexts(8 * BLOCKS - 1, 1, C - 1)
            turn_ctx("tail", 1, 8 * BLOCKS - 2, 0)
            for n in range(0, 4):
                turn_weights(n)
            turn_ctx("tail", 2, 8 * BLOCKS - 1, 1)
            for n in range(4, 8):
                turn_weights(n)
            project_out("tail")
            for n in range(8, 12):
                turn_weights(n)
            turn_attn("tail")
            for n in range(12, 16):
                turn_weights(n)
            turn_x1("tail", BLOCKS - 1)
            affinities("tail")
            ranks("tail", BLOCKS - 1)
            b = fill_work("tail", "count")
            pe.matmul(ps_work[:, b, 0:E], ones[:], seen[:, BLOCK_TILES, :], start=True, stop=True).then_inc(work_filled[b], 1)

            def turn_n(j):
                pe.wait_ge(nrm_ready, j + 1)
                if j >= 2:
                    pe.wait_ge(hin_ready, j - 1)
                pe.transpose(ps_work[:, j % 2, 0:P], nrm[:, j % 2, :], ident[:]).then_inc(nT_filled, 1)

            def up(j):
                pe.wait_ge(hin_ready, j + 1)
                if j >= 2:
                    pe.wait_ge(hT_ready, FK * (j - 1))
                for k in range(FK):
                    last = pe.matmul(ps_scores[:, j % 2, k * P:(k + 1) * P], wst[:, j % 2, k * P:(k + 1) * P],
                                     hin[:, j % 2, :], start=True, stop=True)
                last.then_inc(h_filled, 1)

            def down(j):
                e = pe.value_load(table[0:1, 0, j:j + 1], min_val=0, max_val=E - 1)
                pe.wait_ge(hT_ready, FK * (j + 1))
                if j >= 2:
                    pe.wait_ge(f_drained, j - 1)
                for k in range(FK):
                    last = pe.matmul(ps_scores[:, 2 + j % 2, 0:D], hT[:, j % 2, k * P:(k + 1) * P],
                                     w2T[:, bass.ds(e * F + k * P, D)], start=(k == 0), stop=(k == FK - 1))
                last.then_inc(f_filled, 1)

            pe.wait_ge(turn_drained, 2 * E)
            pe.wait_ge(table_ready, 1)
            for j in range(-1, TILES + 1):
                if j + 1 < TILES:
                    turn_n(j + 1)
                if 0 <= j < TILES:
                    up(j)
                if j >= 1:
                    down(j - 1)


_INS = ['L0_attn_states', 'L0_attn_Wq', 'L0_attn_bq', 'L0_attn_Wk', 'L0_attn_bk', 'L0_attn_Wv', 'L0_attn_bv',
        'L0_attn_Wo', 'L0_attn_bo', 'L0_ffn_centroids', 'L0_ffn_ln_g', 'L0_ffn_ln_b', 'L0_ffn_w1', 'L0_ffn_b1',
        'L0_ffn_w2', 'L0_ffn_b2']
_OUTS = [((8, 256, 128), 'float32')]


def kernel(**inputs):
    import numpy as _np
    import concourse.bacc as _bacc
    from concourse import mybir as _mybir
    from concourse.bass_utils import run_bass_kernel_spmd as _run

    nc = _bacc.Bacc("TRN2", target_bir_lowering=False, num_devices=1)
    arrays, args = {}, []
    for name in _INS:
        a = _np.ascontiguousarray(inputs[name])
        arrays[f"in_{name}_dram"] = a
        args.append(nc.dram_tensor(f"in_{name}_dram", a.shape, _mybir.dt.from_np(a.dtype), kind="ExternalInput").ap())
    for i, (shape, dtype) in enumerate(_OUTS):
        dt = _mybir.dt.from_np(_np.dtype(dtype))
        args.append(nc.dram_tensor(f"out_{i}_dram", shape, dt, kind="ExternalOutput").ap())
    attention_moe(nc, *args)
    r = _run(nc, [arrays], core_ids=[0])
    got = tuple(r.results[0][f"out_{i}_dram"] for i in range(len(_OUTS)))
    return got[0]
```

```python
import math
from contextlib import ExitStack

import concourse.bass as bass
from concourse import mybir
from concourse.alu_op_type import AluOpType as ALU

ACT = mybir.ActivationFunctionType
AX = mybir.AxisListType
F32 = mybir.dt.float32
F32R = mybir.dt.float32r
BF16 = mybir.dt.bfloat16
F16 = mybir.dt.float16
I32 = mybir.dt.int32
U32 = mybir.dt.uint32

P = 128
EPS = 1e-5
BLOCK_TILES = 4
BLOCK = BLOCK_TILES * P
PAD_TILES = 8
ROW = P + 4
ALPHA, TOKEN, MEAN, RSTD = P, P + 1, P + 2, P + 3
LOADS = 8
RING = 4


PROB_FACTOR = 16.0
VALUE_FACTOR = 4096.0


def work_plan(first):
    plan = []
    for i in range(8):
        if i == 0:
            plan.append(("xT", 0))
        plan += [("q", i), ("k", i)]
        if i == 3 and not first:
            plan.append(("proj", 0))
        if i >= 3 or not first:
            plan.append(("ctxT", i))
        if i == 1:
            plan += [("v", u) for u in range(4)]
        if 2 <= i <= 5:
            plan.append(("v", i + 2))
        if not first:
            plan += {4: [("attn", 0)], 5: [("x1T", 0)], 6: [("aff", 0)], 7: [("rank", 0)]}.get(i, [])
    return plan


TAIL_PLAN = [("ctxT", 0), ("ctxT", 1), ("ctxT", 2), ("proj", 0), ("attn", 0), ("x1T", 0), ("aff", 0),
             ("rank", 0), ("count", 0)]


def attention_moe(nc, x, Wq, bq, Wk, bk, Wv, bv, Wo, bo, cen, ln_g, ln_b, w1, b1, w2, b2, out):
    B, S, D = x.shape
    HD = Wq.shape[1]
    E, F, _ = w1.shape
    N = B * S
    DH = 64
    C = HD // P
    BLOCKS = N // BLOCK
    FK = F // P
    TILES = N // P + E
    DV = DH + 1
    WBC = F + FK + 2
    SLOTS = E * N + PAD_TILES * P
    assert (S, D, DH * 2, C, BLOCK) == (2 * P, P, P, 8, 2 * S) and TILES % LOADS == 0

    slots = nc.dram_tensor("slots", [SLOTS, ROW], F32, kind="Internal").ap()
    x_rows = x.rearrange("b s d -> (b s) d")
    out_rows = out.rearrange("b s d -> (b s) d")

    with ExitStack() as ctx:
        def sb(name, shape, dt=F32):
            return ctx.enter_context(nc.sbuf_tensor(name, shape, dt))

        def sem(name):
            return ctx.enter_context(nc.semaphore(name))

        ps_scores = ctx.enter_context(nc.psum_tensor("ps_scores", [P, 4, 512], F32))
        ps_ctx = ctx.enter_context(nc.psum_tensor("ps_ctx", [P, 2, 512], F32))
        ps_work = ctx.enter_context(nc.psum_tensor("ps_work", [P, 2, 512], F32))

        ident = sb("ident", [P, P])
        seen_keys = sb("seen_keys", [P, P])
        before = sb("before", [P, P], BF16)
        ones = sb("ones", [P, P], BF16)
        ones_rows = sb("ones_rows", [64, P], F32R)
        region = sb("region", [P, E])
        expert_ids = sb("expert_ids", [P, E])
        thresholds = sb("thresholds", [P, 16])
        upto = sb("upto", [P, E, E])
        tile_ids = sb("tile_ids", [P, TILES])
        fill = sb("fill", [P, ROW])
        small_rows = sb("small_rows", [P, P])
        small = sb("small", [P, P])
        bv_parts = sb("bv_parts", [64, HD], F32R)
        b2_all = sb("b2_all", [P, E, D])
        x_in = sb("x_in", [P, BLOCK_TILES, D])
        x_res = sb("x_res", [P, BLOCK_TILES, D])
        xT_hi = sb("xT_hi", [P, BLOCK], F32R)
        xT_lo = sb("xT_lo", [P, BLOCK], F32R)
        w_hi = [sb(f"w_hi{n}", [P, HD], F32R) for n in range(4)]
        w_lo = [sb(f"w_lo{n}", [P, HD], F32R) for n in range(4)]
        w2T = sb("w2T", [P, E * F])
        qT, kT, v32 = (w2T[:, n * 2 * BLOCK:(n + 1) * 2 * BLOCK].rearrange("p (a c) -> p a c", a=2) for n in range(3))
        v_hi = sb("v_hi", [P, BLOCK_TILES, 2 * C, DV], F16)
        v_lo = sb("v_lo", [P, BLOCK_TILES, 2 * C, DH], F16)
        p_hi = sb("p_hi", [P, 2, 3 * BLOCK], F16)
        p_lo = sb("p_lo", [P, 2, 3 * BLOCK], F16)
        log_factor = sb("log_factor", [P, 1])
        probs = sb("probs", [P, 2, 3 * BLOCK])
        rden = sb("rden", [P, 2, BLOCK_TILES, 1])
        ctxn = sb("ctxn", [P, 2, BLOCK_TILES, 2, DH])
        cT_hi = sb("cT_hi", [P, C, BLOCK], F32R)
        cT_lo = sb("cT_lo", [P, C, BLOCK], F32R)
        aT = sb("aT", [P, BLOCK])
        bv_row = probs[0:1, 0, 0:HD]
        y = sb("y", [P, BLOCK_TILES, D])
        stats = sb("stats", [P, BLOCK_TILES, 6])
        mv = sb("mv", [P, BLOCK_TILES, 2])
        var_eps = sb("var_eps", [P, BLOCK_TILES, 1])
        minus_half = sb("minus_half", [P, BLOCK_TILES, 1])
        rstd = sb("rstd", [P, BLOCK_TILES, 1])
        pay = sb("pay", [P, BLOCK_TILES, ROW])
        x1T = sb("x1T", [P, BLOCK])
        cenT = sb("cenT", [P, E])
        aff = sb("aff", [P, BLOCK_TILES, E])
        top = sb("top", [P, BLOCK_TILES, 8])
        top_at = sb("top_at", [P, BLOCK_TILES, 8], U32)
        top_f = sb("top_f", [P, BLOCK_TILES, 1])
        exp_neg = sb("exp_neg", [P, BLOCK_TILES, 1])
        exp_one = sb("exp_one", [P, BLOCK_TILES, 1])
        chosen = sb("chosen", [P, BLOCK_TILES, E], BF16)
        seen = sb("seen", [P, BLOCK_TILES + 1, E], BF16)
        slot8 = sb("slot8", [P, BLOCK_TILES, E])
        slot8c = sb("slot8c", [P, BLOCK_TILES, E])
        slot_f = sb("slot_f", [P, BLOCK_TILES, 1])
        slot_i = sb("slot_i", [P, BLOCK_TILES], U32)
        token_f = sb("token_f", [P, BLOCK_TILES, 1])
        w1n = sb("w1n", [P, E * FK, D])
        w2n = sb("w2n", [P, E, F])
        wb = sb("wb", [P, E * WBC])
        stage = wb[:, 0:4 * HD]
        n_e = sb("n_e", [P, E])
        over = sb("over", [P, E, 16])
        tiles_e = sb("tiles_e", [P, E])
        ends8 = sb("ends8", [P, E, E])
        ends = sb("ends", [P, E])
        past = sb("past", [P, TILES, E])
        past_t = sb("past_t", [P, TILES, E])
        exp_of = sb("exp_of", [P, TILES])
        skipped = sb("skipped", [P, TILES])
        row_of = sb("row_of", [P, TILES])
        row_of2 = sb("row_of2", [P, TILES])
        table = sb("table", [P, 2, TILES], I32)
        free = [w1n[:].rearrange("p n d -> p (n d)"), w2n[:].rearrange("p n d -> p (n d)")]
        taken = [0, 0]

        def over_weights(side, parts, width):
            at = taken[side]
            taken[side] += parts * width
            return free[side][:, at:taken[side]].rearrange("p (a d) -> p a d", a=parts)

        wst = over_weights(0, RING, WBC)
        xx = over_weights(0, RING, D)
        fin = over_weights(0, RING, D)
        xg = over_weights(1, LOADS, ROW)
        nrm = over_weights(1, 2, D)
        hin = over_weights(1, 2, P)
        hT = over_weights(1, 2, FK * P)
        fy = over_weights(1, 2, D)
        fz = over_weights(1, 2, D)
        sd3 = sb("sd3", [P, 2, 1])
        st3 = sb("st3", [P, 2, 6])
        mv3 = sb("mv3", [P, 2, 2])
        rs3 = sb("rs3", [P, 2, 1])
        eps = sb("eps", [P, 1])

        consts_ready = sem("consts_ready")
        memset_done = sem("memset_done")
        x_loaded = sem("x_loaded")
        xres_loaded = sem("xres_loaded")
        wproj_loaded = [sem(f"wproj_loaded{n}") for n in range(4)]
        small_loaded = sem("small_loaded")
        wffn_loaded = sem("wffn_loaded")
        small_turned = sem("small_turned")
        small_ready = sem("small_ready")
        slots_filled = sem("slots_filled")
        wproj_split = sem("wproj_split")
        pool_step = sem("pool_step")
        dve_step = sem("dve_step")
        work_filled = [sem(f"work_filled{b}") for b in range(2)]
        work_drained = [sem(f"work_drained{b}") for b in range(2)]
        scores_ready = sem("scores_ready")
        exp_done = sem("exp_done")
        probs_masked = sem("probs_masked")
        p_hi_ready = sem("p_hi_ready")
        probs_ready = sem("probs_ready")
        v_split = sem("v_split")
        ctx_ready = sem("ctx_ready")
        ctx_normed = sem("ctx_normed")
        y_ready = sem("y_ready")
        var_ready = sem("var_ready")
        rstd_ready = sem("rstd_ready")
        mvout_ready = sem("mvout_ready")
        sdout_ready = sem("sdout_ready")
        x1_ready = sem("x1_ready")
        x1T_ready = sem("x1T_ready")
        top_ready = sem("top_ready")
        expneg_ready = sem("expneg_ready")
        chosen_ready = sem("chosen_ready")
        slot_ready = sem("slot_ready")
        scatter_begun = sem("scatter_begun")
        scattered = sem("scattered")
        turned = sem("turned")
        turn_drained = sem("turn_drained")
        table_ready = sem("table_ready")
        slots_loaded = [sem(f"slots_loaded{n}") for n in range(LOADS)]
        wst_loaded = [sem(f"wst_loaded{n}") for n in range(RING)]
        fz_ready = sem("fz_ready")
        st3_ready = sem("st3_ready")
        rs3_ready = sem("rs3_ready")
        nrm_ready = sem("nrm_ready")
        twice_ready = sem("twice_ready")
        nT_filled = sem("nT_filled")
        hin_ready = sem("hin_ready")
        h_filled = sem("h_filled")
        hT_ready = sem("hT_ready")
        f_filled = sem("f_filled")
        f_drained = sem("f_drained")
        fin_ready = sem("fin_ready")
        stored = [sem(f"stored{n}") for n in range(LOADS)]

        first_plan, steady_plan = work_plan(True), work_plan(False)
        assert len(first_plan) % 2 == 0 and len(steady_plan) % 2 == 0

        def work(s, kind, i=0):
            if isinstance(s, str):
                plan, base = TAIL_PLAN, (len(first_plan) + (BLOCKS - 1) * len(steady_plan)) // 2
            elif isinstance(s, int) and s == 0:
                plan, base = first_plan, 0
            else:
                plan, base = steady_plan, (s - 1) * (len(steady_plan) // 2) + len(first_plan) // 2
            k = plan.index((kind, i))
            return k % 2, base + (k // 2 + 1)

        def wait(eng, s, value):
            if isinstance(value, int) and value <= 0:
                return
            eng.wait_ge(s, value)

        BQ, BK, BO, B1, LG, LB, CEN = 0, C, 2 * C, 2 * C + 1, 2 * C + 1 + E * FK, 2 * C + 1 + E * FK + E, 2 * C + 1 + E * FK + 2 * E
        SMALL = CEN + E
        N_SMALL = 7

        block = ctx.enter_context(nc.Block())

        @block.sync
        def _(sp):
            def x_tiles(s):
                return x_rows[bass.ds(s * BLOCK, BLOCK), :].rearrange("(t p) d -> p t d", p=P)

            sp.dma_start(x_in[:], x_tiles(0)).then_inc(x_loaded, 16)
            for n, w in enumerate((Wq, Wk, Wv)):
                sp.dma_start(stage[:, n * HD:(n + 1) * HD], w).then_inc(wproj_loaded[n], 16)
            sp.dma_start(stage[:, 3 * HD:4 * HD].rearrange("p (c d) -> p c d", c=C),
                         Wo.rearrange("(c p) d -> p c d", p=P)).then_inc(wproj_loaded[3], 16)
            sp.wait_ge(exp_done, 2)
            sp.dma_start(w1n[:].rearrange("p (e k) d -> p e k d", e=E),
                         w1.rearrange("e (k p) d -> p e k d", p=P)).then_inc(wffn_loaded, 16)
            sp.dma_start(w2n[:], w2.rearrange("e d f -> d e f")).then_inc(wffn_loaded, 16)
            sp.dma_start(b2_all[:].rearrange("p e d -> p (e d)"),
                         b2.rearrange("e d -> (e d)").partition_broadcast(P)).then_inc(wffn_loaded, 16)
            sp.wait_ge(consts_ready, 1)
            tiles = SLOTS // P
            per = tiles // 4
            view = slots.rearrange("(n p) c -> p n c", p=P)
            for n in range(4):
                sp.dma_start(view[:, n * per:(n + 1) * per, :],
                             fill[:].unsqueeze(1).broadcast_to([P, per, ROW])).then_inc(slots_filled, 16)

            def body(s):
                b, n = work(s - 1, "xT")
                sp.wait_ge(work_drained[b], n)
                sp.dma_start(x_in[:], x_tiles(s)).then_inc(x_loaded, 16)
                wait(sp, y_ready, s - 1)
                sp.dma_start(x_res[:], x_tiles(s - 1)).then_inc(xres_loaded, 16)

            body(1)
            with sp.Fori(2, BLOCKS) as s:
                body(s)
            sp.wait_ge(y_ready, BLOCKS - 1)
            sp.dma_start(x_res[:], x_tiles(BLOCKS - 1)).then_inc(xres_loaded, 16)

            sp.wait_ge(table_ready, 1)
            sp.wait_ge(scattered, 16 * BLOCKS * BLOCK_TILES)
            sp.wait_ge(turn_drained, 2 * E)
            for j in range(TILES):
                row = sp.value_load(table[0:1, 1, j:j + 1], min_val=0, max_val=SLOTS - P)
                e = sp.value_load(table[0:1, 0, j:j + 1], min_val=0, max_val=E - 1)
                if j >= LOADS:
                    sp.wait_ge(stored[j % LOADS], 16 * (j // LOADS))
                sp.dma_start(xg[:, j % LOADS, :], slots[bass.ds(row, P), :]).then_inc(slots_loaded[j % LOADS], 16)
                if j >= RING:
                    sp.wait_ge(hT_ready, FK * (j - RING + 1))
                sp.dma_start(wst[:, j % RING, :], wb[:, bass.ds(e * WBC, WBC)]).then_inc(wst_loaded[j % RING], 16)

        @block.gpsimd
        def _(pool):
            count = [0]

            def link(ins):
                count[0] += 1
                ins.then_inc(pool_step, 1)
                pool.wait_ge(pool_step, count[0])

            pool.memset(small_rows[:], 0.0).then_inc(memset_done, 1)
            link(pool.memset(fill[:], 0.0))
            link(pool.iota(fill[:].bitcast(I32)[:, TOKEN:TOKEN + 1], pattern=[[0, 1]], base=N, channel_multiplier=1))
            pool.nop().then_inc(consts_ready, 1)
            link(pool.memset(ident[:], 0.0))
            link(pool.affine_select(out=ident[:], in_=ident[:], compare_op=ALU.not_equal, fill=1.0, base=0,
                                    pattern=[[-1, P]], channel_multiplier=1))
            link(pool.memset(ones[:], 1.0))
            link(pool.affine_select(out=before[:], in_=ones[:], compare_op=ALU.is_gt, fill=0.0, base=0,
                                    pattern=[[1, P]], channel_multiplier=-1))
            link(pool.memset(seen_keys[:], 1.0))
            link(pool.affine_select(out=seen_keys[:], in_=seen_keys[:], compare_op=ALU.is_ge, fill=0.0, base=0,
                                    pattern=[[1, P]], channel_multiplier=-1))
            pool.iota(region[:], pattern=[[N, E]], base=0, channel_multiplier=0, allow_small_or_imprecise_dtypes=True)
            pool.iota(expert_ids[:], pattern=[[1, E]], base=0, channel_multiplier=0, allow_small_or_imprecise_dtypes=True)
            pool.iota(thresholds[:], pattern=[[P, 16]], base=0, channel_multiplier=0, allow_small_or_imprecise_dtypes=True)
            pool.iota(tile_ids[:], pattern=[[1, TILES]], base=0, channel_multiplier=0, allow_small_or_imprecise_dtypes=True)
            pool.iota(token_f[:], pattern=[[P, BLOCK_TILES]], base=0, channel_multiplier=1, allow_small_or_imprecise_dtypes=True)
            link(pool.memset(upto[:], 1.0))
            link(pool.affine_select(out=upto[:], in_=upto[:], compare_op=ALU.is_ge, fill=0.0, base=0,
                                    pattern=[[1, E], [-1, E]], channel_multiplier=0))
            link(pool.memset(v_hi[:, :, :, DH:DV], VALUE_FACTOR))
            link(pool.memset(log_factor[:], math.log(PROB_FACTOR)))
            link(pool.memset(pay[:], 0.0))
            link(pool.memset(minus_half[:], -0.5))
            link(pool.memset(eps[:], EPS))
            link(pool.memset(bv_parts[:].bitcast(F32), 0.0))
            link(pool.memset(ones_rows[:].bitcast(F32), 1.0))
            pool.nop().then_inc(consts_ready, 1)

            def mask(g, par):
                for part, (start, end, step) in enumerate(((0, 2 * BLOCK, S), (2 * BLOCK, 3 * BLOCK, P))):
                    pool.wait_ge(exp_done, 2 * g + part + 1)
                    v = probs[:, par, start:end].rearrange("p (n q) -> p n q", q=step)[:, :, 0:P]
                    pool.tensor_tensor(v, v, seen_keys[:].unsqueeze(1).broadcast_to([P, 4, P]),
                                       ALU.mult).then_inc(probs_masked, 1)

            def root(b, inner):
                pool.wait_ge(var_ready, 2 * b + inner + 1)
                pool.tensor_tensor(pay[:, :, RSTD:RSTD + 1] if inner else rstd[:], var_eps[:], minus_half[:],
                                   ALU.pow).then_inc(rstd_ready, 1)

            def scatter(b):
                pool.wait_ge(slot_ready, b + 1)
                pool.sem_inc(scatter_begun, 1)
                for t in range(BLOCK_TILES):
                    pool.indirect_dma_start(slots, bass.IndirectOffsetOnAxis(ap=slot_i[:, t:t + 1], axis=0),
                                            pay[:, t, :], None, bounds_check=SLOTS - 1,
                                            oob_is_err=False).then_inc(scattered, 16)

            def body(s, first=False):
                for i in range(8):
                    if i or not first:
                        mask(8 * s - 1 + i, (i + 1) % 2)
                    if i == 4 and not first:
                        root(s - 1, 0)
                    if i == 5 and not first:
                        root(s - 1, 1)
                if not first:
                    scatter(s - 1)

            body(0, True)
            pool.wait_ge(slots_filled, 64)
            with pool.Fori(1, BLOCKS) as s:
                body(s)
            mask(8 * BLOCKS - 1, 1)
            root(BLOCKS - 1, 0)
            root(BLOCKS - 1, 1)
            scatter(BLOCKS - 1)

            for j in range(TILES):
                pool.wait_ge(fin_ready, j + 1)
                pool.indirect_dma_start(out_rows, bass.IndirectOffsetOnAxis(
                    ap=xg.bitcast(U32)[:, j % LOADS, TOKEN:TOKEN + 1], axis=0), fin[:, j % RING, :], None,
                    bounds_check=N - 1, oob_is_err=False).then_inc(stored[j % LOADS], 16)
            for q in range(LOADS):
                pool.wait_ge(stored[q], 16 * (TILES // LOADS))

        @block.scalar
        def _(act):
            def tanh_qk(s, i):
                par = i % 2
                for kind, dst, base in (("q", qT, BQ), ("k", kT, BK)):
                    b, n = work(s, kind, i)
                    act.wait_ge(work_filled[b], n)
                    act.activation(dst[:, par, :], ps_work[:, b, :], ACT.Tanh,
                                   bias=small[:, base + i:base + i + 1]).then_inc(work_drained[b], 1)

            def tanh_v(s, u):
                b, n = work(s, "v", u)
                act.wait_ge(work_filled[b], n)
                wait(act, v_split, 8 * s + u - 1)
                act.activation(v32[:, u % 2, :], ps_work[:, b, :], ACT.Tanh).then_inc(work_drained[b], 1)

            def high_probs(g, par):
                for part, cols in enumerate((slice(0, 2 * BLOCK), slice(2 * BLOCK, 3 * BLOCK))):
                    act.wait_ge(probs_masked, 2 * g + part + 1)
                    act.copy(p_hi[:, par, cols], probs[:, par, cols]).then_inc(p_hi_ready, 1)

            def exp_scores(g, par):
                act.wait_ge(scores_ready, g + 1)
                ps = ps_scores[:].rearrange("p (h z) c -> p h z c", h=2)
                act.activation(probs[:, par, 0:2 * BLOCK].rearrange("p (h c) -> p h c", h=2), ps[:, :, 0, :],
                               ACT.Exp, scale=DH ** -0.5, bias=log_factor[:]).then_inc(exp_done, 1)
                act.activation(probs[:, par, 2 * BLOCK:3 * BLOCK].rearrange("p (h c) -> p h c", h=2),
                               ps[:, :, 1, 0:S], ACT.Exp, scale=DH ** -0.5, bias=log_factor[:]).then_inc(exp_done, 1)

            def tanh_out(s):
                b, n = work(s, "proj")
                act.wait_ge(work_filled[b], n)
                act.activation(aT[:], ps_work[:, b, :], ACT.Tanh, bias=small[:, BO:BO + 1]).then_inc(work_drained[b], 1)

            def copy_x1T(s):
                b, n = work(s, "x1T")
                act.wait_ge(work_filled[b], n)
                act.copy(x1T[:], ps_work[:, b, :]).then_inc(work_drained[b], 1)

            def exp_gate(blk):
                act.wait_ge(top_ready, blk + 1)
                act.activation(exp_neg[:], top[:, :, 0:1], ACT.Exp, scale=-1.0).then_inc(expneg_ready, 1)

            def body(s, first=False):
                for i in range(8):
                    if i or not first:
                        exp_scores(8 * s - 1 + i, (i + 1) % 2)
                    tanh_qk(s, i)
                    if i == 3 and not first:
                        tanh_out(s)
                    if i or not first:
                        high_probs(8 * s - 1 + i, (i + 1) % 2)
                    if i == 1:
                        for u in range(4):
                            tanh_v(s, u)
                    if 2 <= i <= 5:
                        tanh_v(s, i + 2)
                    if i == 5 and not first:
                        copy_x1T(s)
                    if i == 7 and not first:
                        exp_gate(s - 1)

            act.wait_ge(memset_done, 1)
            for row, n, src in ((BQ, C, bq.rearrange("(c p) -> c p", p=P)), (BK, C, bk.rearrange("(c p) -> c p", p=P)),
                                (BO, 1, bo.rearrange("(c p) -> c p", p=P)), (B1, E * FK, b1.rearrange("e (k p) -> (e k) p", p=P)),
                                (LG, E, ln_g), (LB, E, ln_b), (CEN, E, cen)):
                act.dma_start(small_rows[row:row + n, :], src).then_inc(small_loaded, 16)
            act.dma_start(bv_row, bv.rearrange("(o n) -> o n", o=1)).then_inc(small_loaded, 16)
            act.wait_ge(small_turned, 1)
            act.copy(small[:, 0:SMALL], ps_ctx[:, 0, 0:SMALL]).then_inc(small_ready, 1)
            act.wait_ge(small_ready, 1)
            body(0, True)
            with act.Fori(1, BLOCKS) as s:
                body(s)
            exp_scores(8 * BLOCKS - 1, 1)
            high_probs(8 * BLOCKS - 1, 1)

            wbv = wb[:].rearrange("p (e c) -> p e c", e=E)

            def drain_turned(n):
                act.wait_ge(turned, n + 1)
                dst = wbv[:, n, 0:F] if n < E else w2T[:, (n - E) * F:(n - E + 1) * F]
                act.copy(dst, ps_scores[:, n % 4, :]).then_inc(turn_drained, 1)

            for n in range(8):
                drain_turned(n)
            tanh_out("tail")
            for n in range(8, 12):
                drain_turned(n)
            copy_x1T("tail")
            for n in range(12, 16):
                drain_turned(n)
            exp_gate(BLOCKS - 1)

            def relu(j):
                act.wait_ge(h_filled, j + 1)
                for k in range(FK):
                    act.activation(hT[:, j % 2, k * P:(k + 1) * P], ps_scores[:, j % 2, k * P:(k + 1) * P], ACT.Relu,
                                   bias=wst[:, j % RING, F + k:F + k + 1]).then_inc(hT_ready, 1)

            def twice(j):
                act.wait_ge(slots_loaded[j % LOADS], 16 * (j // LOADS + 1))
                act.mul(xx[:, j % RING, :], xg[:, j % LOADS, 0:D], 2.0).then_inc(twice_ready, 1)

            def deviation(j):
                act.wait_ge(mvout_ready, j + 1)
                act.activation(sd3[:, j % 2, :], mv3[:, j % 2, 1:2], ACT.Sqrt, bias=eps[:]).then_inc(sdout_ready, 1)

            for j in range(TILES + 3):
                if j < TILES:
                    relu(j)
                    twice(j)
                if 2 <= j < TILES + 2:
                    deviation(j - 2)

        @block.vector
        def _(dve):
            count = [0]

            def link(ins):
                count[0] = count[0] + 1
                ins.then_inc(dve_step, 1)
                dve.wait_ge(dve_step, count[0])

            dve.wait_ge(consts_ready, 2)
            dve.wait_ge(small_loaded, 16 * (N_SMALL + 1))
            link(dve.tensor_copy(bv_parts[0:1, :], bv_row))
            dve.tensor_tensor(bv_parts[32:33, :], bv_row, bv_parts[0:1, :], ALU.subtract).then_inc(wproj_split, 1)
            for n in range(3):
                dve.wait_ge(wproj_loaded[n], 16)
                src = stage[:, n * HD:(n + 1) * HD]
                link(dve.tensor_copy(w_hi[n][:], src))
                dve.tensor_tensor(w_lo[n][:], src, w_hi[n][:], ALU.subtract).then_inc(wproj_split, 1)
            def split_xT(s):
                b, n = work(s, "xT")
                dve.wait_ge(work_filled[b], n)
                link(dve.tensor_copy(xT_hi[:], ps_work[:, b, :]))
                dve.tensor_tensor(xT_lo[:], ps_work[:, b, :], xT_hi[:], ALU.subtract).then_inc(work_drained[b], 1)

            def normalise(g, par):
                dve.wait_ge(ctx_ready, g + 1)
                c = ps_ctx[:, :, 0:BLOCK_TILES * DV].rearrange("p h (t e) -> p h t e", e=DV)
                link(dve.reciprocal(rden[:], c[:, :, :, DH:DV]))
                dve.tensor_tensor(ctxn[:, par].rearrange("p t h d -> p h t d"), c[:, :, :, 0:DH],
                                  rden[:].broadcast_to([P, 2, BLOCK_TILES, DH]), ALU.mult).then_inc(ctx_normed, 1)

            def low_probs(g, par):
                for part, cols in enumerate((slice(0, 2 * BLOCK), slice(2 * BLOCK, 3 * BLOCK))):
                    dve.wait_ge(p_hi_ready, 2 * g + part + 1)
                    dve.tensor_tensor(p_lo[:, par, cols], probs[:, par, cols], p_hi[:, par, cols],
                                      ALU.subtract).then_inc(probs_ready, 1)

            def split_v(s, u):
                b, n = work(s, "v", u)
                t, heads = u % 4, slice(u // 4 * C, (u // 4 + 1) * C)
                dve.wait_ge(work_drained[b], n)
                src, hi = v32[:, u % 2, :].rearrange("p (h d) -> p h d", d=DH), v_hi[:, t, heads, 0:DH]
                link(dve.tensor_scalar(hi, src, VALUE_FACTOR, None, ALU.mult))
                dve.scalar_tensor_tensor(out=v_lo[:, t, heads, :], in0=src, scalar=VALUE_FACTOR, in1=hi,
                                         op0=ALU.mult, op1=ALU.subtract).then_inc(v_split, 1)

            def split_cT(s, i, c):
                b, n = work(s, "ctxT", i)
                dve.wait_ge(work_filled[b], n)
                link(dve.tensor_copy(cT_hi[:, c, :], ps_work[:, b, :]))
                dve.tensor_tensor(cT_lo[:, c, :], ps_work[:, b, :], cT_hi[:, c, :], ALU.subtract).then_inc(work_drained[b], 1)

            def layer_norm_1(s, blk):
                b, n = work(s, "attn")
                dve.wait_ge(work_filled[b], n)
                dve.wait_ge(xres_loaded, 16 * (blk + 1))
                dve.tensor_tensor(y[:].rearrange("p t d -> p (t d)"), ps_work[:, b, :],
                                  x_res[:].rearrange("p t d -> p (t d)"), ALU.add).then_inc(work_drained[b], 1)
                dve.wait_ge(work_drained[b], n)
                for t in range(BLOCK_TILES):
                    last = dve.bn_stats(stats[:, t, :], y[:, t, :])
                link(last)
                dve.sem_inc(y_ready, 1)
                for t in range(BLOCK_TILES):
                    last = dve.bn_aggr(mv[:, t, :], stats[:, t, :])
                link(last)
                dve.tensor_scalar(var_eps[:], mv[:, :, 1:2], EPS, None, ALU.add).then_inc(var_ready, 1)
                dve.wait_ge(rstd_ready, 2 * blk + 1)
                wait(dve, scattered, 16 * BLOCK_TILES * blk)
                for t in range(BLOCK_TILES):
                    last = dve.tensor_scalar(pay[:, t, 0:D], y[:, t, :], mv[:, t, 0:1], rstd[:, t, :],
                                             ALU.subtract, ALU.mult)
                last.then_inc(x1_ready, 1)

            def inner_stats(blk):
                dve.wait_ge(x1_ready, blk + 1)
                for t in range(BLOCK_TILES):
                    last = dve.bn_stats(stats[:, t, :], pay[:, t, 0:D])
                link(last)
                for t in range(BLOCK_TILES):
                    last = dve.bn_aggr(mv[:, t, :], stats[:, t, :])
                link(last)
                dve.tensor_copy(pay[:, :, MEAN:MEAN + 1], mv[:, :, 0:1])
                dve.tensor_scalar(var_eps[:], mv[:, :, 1:2], EPS, None, ALU.add).then_inc(var_ready, 1)

            def choose(s, blk):
                b, n = work(s, "aff")
                dve.wait_ge(work_filled[b], n)
                dve.tensor_copy(aff[:].rearrange("p t e -> p (t e)"),
                                ps_work[:, b, 0:BLOCK_TILES * E]).then_inc(work_drained[b], 1)
                dve.wait_ge(work_drained[b], n)
                for t in range(BLOCK_TILES):
                    last = dve.max(top[:, t, :], aff[:, t, :])
                last.then_inc(top_ready, 1)
                dve.wait_ge(top_ready, blk + 1)
                for t in range(BLOCK_TILES):
                    last = dve.max_index(top_at[:, t, :], top[:, t, :], aff[:, t, :])
                link(last)
                link(dve.tensor_copy(top_f[:], top_at[:, :, 0:1]))
                dve.tensor_copy(seen[:, 0, :], seen[:, BLOCK_TILES, :])
                link(dve.tensor_tensor(chosen[:], expert_ids[:].unsqueeze(1).broadcast_to([P, BLOCK_TILES, E]),
                                       top_f[:].broadcast_to([P, BLOCK_TILES, E]), ALU.is_equal))
                for t in range(BLOCK_TILES):
                    link(dve.tensor_tensor(seen[:, t + 1, :], seen[:, t, :], chosen[:, t, :], ALU.add))
                dve.sem_inc(chosen_ready, 1)

            def place(s, blk):
                b, n = work(s, "rank")
                dve.wait_ge(rstd_ready, 2 * blk + 2)
                dve.wait_ge(expneg_ready, blk + 1)
                link(dve.tensor_scalar(exp_one[:], exp_neg[:], 1.0, None, ALU.add))
                dve.reciprocal(pay[:, :, ALPHA:ALPHA + 1], exp_one[:])
                dve.tensor_copy(pay[:].bitcast(I32)[:, :, TOKEN:TOKEN + 1], token_f[:])
                dve.wait_ge(work_filled[b], n)
                dve.tensor_tensor(slot8[:], ps_work[:, b, 0:BLOCK_TILES * E].rearrange("p (t e) -> p t e", e=E),
                                  region[:].unsqueeze(1).broadcast_to([P, BLOCK_TILES, E]),
                                  ALU.add).then_inc(work_drained[b], 1)
                dve.wait_ge(work_drained[b], n)
                link(dve.tensor_tensor(slot8c[:], slot8[:], chosen[:], ALU.mult))
                link(dve.tensor_reduce(slot_f[:], slot8c[:], AX.X, ALU.add))
                dve.tensor_scalar(token_f[:], token_f[:], float(BLOCK), None, ALU.add)
                dve.tensor_copy(slot_i[:].unsqueeze(2), slot_f[:]).then_inc(slot_ready, 1)

            def body(s, first=False):
                for i in range(8):
                    if i == 0:
                        split_xT(s)
                    if i == 2 and first:
                        dve.wait_ge(wproj_loaded[3], 16)
                        src = stage[:, 3 * HD:4 * HD]
                        link(dve.tensor_copy(w_hi[3][:], src))
                        dve.tensor_tensor(w_lo[3][:], src, w_hi[3][:], ALU.subtract).then_inc(wproj_split, 1)
                        dve.wait_ge(small_ready, 1)
                        dve.tensor_copy(cenT[:], small[:, CEN:CEN + E])
                        link(dve.memset(seen[:, BLOCK_TILES, :], 0.0))
                    if i >= 2 or not first:
                        normalise(8 * s - 2 + i, i % 2)
                    if i >= 3 or not first:
                        split_cT(s, i, (i + 5) % 8)
                    if i or not first:
                        low_probs(8 * s - 1 + i, (i + 1) % 2)
                    if i == 1:
                        for u in range(4):
                            split_v(s, u)
                    if 2 <= i <= 5:
                        split_v(s, i + 2)
                    if not first:
                        if i == 4:
                            layer_norm_1(s, s - 1)
                        if i == 5:
                            inner_stats(s - 1)
                        if i == 6:
                            choose(s, s - 1)
                        if i == 7:
                            place(s, s - 1)

            body(0, True)
            for s in range(1, BLOCKS):
                body(s)
            normalise(8 * BLOCKS - 2, 0)
            split_cT("tail", 0, C - 3)
            low_probs(8 * BLOCKS - 1, 1)
            normalise(8 * BLOCKS - 1, 1)
            split_cT("tail", 1, C - 2)
            split_cT("tail", 2, C - 1)
            wbv = wb[:].rearrange("p (e c) -> p e c", e=E)
            dve.tensor_copy(wbv[:, :, F:F + FK], small[:, B1:B1 + E * FK].rearrange("p (e k) -> p e k", e=E))
            dve.tensor_copy(wbv[:, :, F + FK:F + FK + 1], small[:, LG:LG + E].unsqueeze(2))
            dve.tensor_copy(wbv[:, :, F + FK + 1:F + FK + 2], small[:, LB:LB + E].unsqueeze(2))
            layer_norm_1("tail", BLOCKS - 1)
            inner_stats(BLOCKS - 1)
            choose("tail", BLOCKS - 1)
            place("tail", BLOCKS - 1)

            b, n = work("tail", "count")
            dve.wait_ge(work_filled[b], n)
            link(dve.tensor_copy(n_e[:], ps_work[:, b, 0:E]))
            link(dve.tensor_tensor(over[:], n_e[:].unsqueeze(2).broadcast_to([P, E, 16]),
                                   thresholds[:].unsqueeze(1).broadcast_to([P, E, 16]), ALU.is_gt))
            link(dve.tensor_reduce(tiles_e[:].unsqueeze(2), over[:], AX.X, ALU.add))
            link(dve.tensor_tensor(ends8[:], upto[:], tiles_e[:].unsqueeze(1).broadcast_to([P, E, E]), ALU.mult))
            link(dve.tensor_reduce(ends[:].unsqueeze(2), ends8[:], AX.X, ALU.add))
            link(dve.tensor_tensor(past[:], tile_ids[:].unsqueeze(2).broadcast_to([P, TILES, E]),
                                   ends[:].unsqueeze(1).broadcast_to([P, TILES, E]), ALU.is_ge))
            dve.tensor_reduce(exp_of[:].unsqueeze(2), past[:], AX.X, ALU.add)
            link(dve.tensor_tensor(past_t[:], past[:], tiles_e[:].unsqueeze(1).broadcast_to([P, TILES, E]), ALU.mult))
            link(dve.tensor_reduce(skipped[:].unsqueeze(2), past_t[:], AX.X, ALU.add))
            link(dve.tensor_tensor(row_of[:], tile_ids[:], skipped[:], ALU.subtract))
            link(dve.tensor_scalar(row_of2[:], row_of[:], float(P), None, ALU.mult))
            dve.tensor_scalar(table[:, 0, :], exp_of[:], float(E - 1), None, ALU.min)
            link(dve.scalar_tensor_tensor(out=table[:, 1, :], in0=exp_of[:], scalar=float(N), in1=row_of2[:],
                                          op0=ALU.mult, op1=ALU.add))
            dve.sem_inc(table_ready, 1)

            def norm_in(j):
                q = j % LOADS
                dve.wait_ge(slots_loaded[q], 16 * (j // LOADS + 1))
                dve.tensor_scalar(nrm[:, j % 2, :], xg[:, q, 0:D], xg[:, q, MEAN:MEAN + 1], xg[:, q, RSTD:RSTD + 1],
                                  ALU.subtract, ALU.mult).then_inc(nrm_ready, 1)

            def scale_in(j):
                p, w = j % 2, wst[:, j % RING, :]
                dve.wait_ge(nT_filled, j + 1)
                dve.wait_ge(wst_loaded[j % RING], 16 * (j // RING + 1))
                dve.tensor_scalar(hin[:, p, :], ps_work[:, p, 0:P], w[:, F + FK:F + FK + 1],
                                  w[:, F + FK + 1:F + FK + 2], ALU.mult, ALU.add).then_inc(hin_ready, 1)

            def add_b2(j):
                e = dve.value_load(table[0:1, 0, j:j + 1], min_val=0, max_val=E - 1)
                dve.wait_ge(f_filled, j + 1)
                dve.tensor_tensor(fy[:, j % 2, :], ps_scores[:, 2 + j % 2, 0:D],
                                  b2_all[:].rearrange("p e d -> p (e d)")[:, bass.ds(e * D, D)],
                                  ALU.add).then_inc(f_drained, 1)

            def residual(j):
                dve.wait_ge(f_drained, j + 1)
                dve.wait_ge(twice_ready, j + 1)
                dve.scalar_tensor_tensor(out=fz[:, j % 2, :], in0=fy[:, j % 2, :],
                                         scalar=xg[:, j % LOADS, ALPHA:ALPHA + 1], in1=xx[:, j % RING, :],
                                         op0=ALU.mult, op1=ALU.add).then_inc(fz_ready, 1)

            def stats_out(j):
                dve.wait_ge(fz_ready, j + 1)
                dve.bn_stats(st3[:, j % 2, :], fz[:, j % 2, :]).then_inc(st3_ready, 1)

            def moments_out(j):
                dve.wait_ge(st3_ready, j + 1)
                dve.bn_aggr(mv3[:, j % 2, :], st3[:, j % 2, :]).then_inc(mvout_ready, 1)

            def inverse_out(j):
                dve.wait_ge(sdout_ready, j + 1)
                dve.reciprocal(rs3[:, j % 2, :], sd3[:, j % 2, :]).then_inc(rs3_ready, 1)

            def norm_out(j):
                p = j % 2
                dve.wait_ge(rs3_ready, j + 1)
                if j >= RING:
                    dve.wait_ge(stored[(j - RING) % LOADS], 16 * ((j - RING) // LOADS + 1))
                dve.tensor_scalar(fin[:, j % RING, :], fz[:, p, :], mv3[:, p, 0:1], rs3[:, p, :], ALU.subtract,
                                  ALU.mult).then_inc(fin_ready, 1)

            for j in range(-2, TILES + 3):
                for stage_of, at in ((scale_in, j + 1), (add_b2, j - 2), (norm_in, j + 2), (inverse_out, j - 3),
                                     (residual, j - 2), (norm_out, j - 3), (stats_out, j - 2), (moments_out, j - 2)):
                    if 0 <= at < TILES:
                        stage_of(at)

        @block.tensor
        def _(pe):
            def fill_work(s, kind, i=0):
                b, n = work(s, kind, i)
                wait(pe, work_drained[b], n - 1)
                return b

            def transposes(b, tiles):
                for t in range(BLOCK_TILES):
                    last = pe.transpose(ps_work[:, b, t * P:(t + 1) * P], tiles[t], ident[:])
                last.then_inc(work_filled[b], 1)

            def product3(o, lhs, rhs, start=True, stop=True):
                pe.matmul(o, lhs[0], rhs[0], start=start, stop=False)
                pe.matmul(o, lhs[0], rhs[1], start=False, stop=False)
                return pe.matmul(o, lhs[1], rhs[0], start=False, stop=stop)

            def turn_x(s):
                pe.wait_ge(x_loaded, 16 * (s + 1))
                b = fill_work(s, "xT")
                transposes(b, [x_in[:, t, :] for t in range(BLOCK_TILES)])

            def drained(s, kind, i=0):
                b, n = work(s, kind, i)
                pe.wait_ge(work_drained[b], n)

            def project_qk(s, i):
                if isinstance(s, int) and i == 0:
                    pe.wait_ge(small_ready, 1)
                for w, kind in enumerate(("q", "k")):
                    if isinstance(s, int) and i == 0:
                        pe.wait_ge(wproj_split, w + 2)
                    b = fill_work(s, kind, i)
                    if i == 0:
                        drained(s, "xT")
                    cols = slice(i * P, (i + 1) * P)
                    product3(ps_work[:, b, :], (w_hi[w][:, cols], w_lo[w][:, cols]),
                             (xT_hi[:], xT_lo[:])).then_inc(work_filled[b], 1)

            def project_v(s, u):
                if isinstance(s, int) and u == 0:
                    pe.wait_ge(wproj_split, 4)
                b = fill_work(s, "v", u)
                t, half = u % 4, u // 4
                toks, cols = slice(t * P, (t + 1) * P), slice(half * 512, (half + 1) * 512)
                pe.matmul(ps_work[:, b, :], ones_rows[:], bv_parts[:, cols], start=True, stop=False)
                product3(ps_work[:, b, :], (xT_hi[:, toks], xT_lo[:, toks]), (w_hi[2][:, cols], w_lo[2][:, cols]),
                         start=False).then_inc(work_filled[b], 1)

            def scores(g, par, s, i):
                if isinstance(s, str):
                    for kind in "qk":
                        b, n = work(BLOCKS - 1, kind, 7)
                        pe.wait_ge(work_drained[b], n)
                elif i:
                    drained(s, "q", i - 1)
                    drained(s, "k", i - 1)
                else:
                    drained_before(s)
                wait(pe, exp_done, 2 * g)
                for bb in range(2):
                    o = bb * S
                    for hh in range(2):
                        rows = slice(hh * DH, (hh + 1) * DH)
                        pe.matmul(ps_scores[:, 2 * hh, o:o + S], kT[rows, par, o:o + P], qT[rows, par, o:o + S],
                                  start=True, stop=True)
                for bb in range(2):
                    o = bb * S + P
                    for hh in range(2):
                        rows = slice(hh * DH, (hh + 1) * DH)
                        last = pe.matmul(ps_scores[:, 2 * hh + 1, bb * P:(bb + 1) * P], kT[rows, par, o:o + P],
                                         qT[rows, par, o:o + P], start=True, stop=True)
                last.then_inc(scores_ready, 1)

            def drained_before(s):
                for kind in "qk":
                    k = steady_plan.index((kind, 7)) - len(steady_plan)
                    base = (s - 1) * (len(steady_plan) // 2) + len(first_plan) // 2
                    pe.wait_ge(work_drained[k % 2], base + (k // 2 + 1))

            def contexts(g, par, pair):
                pe.wait_ge(probs_ready, 2 * (g + 1))
                wait(pe, ctx_normed, g)
                for hh in range(2):
                    h = 2 * pair + hh
                    for bb in range(2):
                        first, second = hh * BLOCK + bb * S, 2 * BLOCK + hh * S + bb * P
                        for qt, kt, at in ((0, 0, first), (1, 0, first + P), (1, 1, second)):
                            cols, tok = slice(at, at + P), 2 * bb + kt
                            o = ps_ctx[:, hh, (2 * bb + qt) * DV:(2 * bb + qt + 1) * DV]
                            pe.matmul(o, p_hi[:, par, cols], v_hi[:, tok, h, :], start=(kt == 0), stop=False)
                            pe.matmul(o[:, 0:DH], p_hi[:, par, cols], v_lo[:, tok, h, :], start=False, stop=False)
                            last = pe.matmul(o, p_lo[:, par, cols], v_hi[:, tok, h, :], start=False,
                                             stop=(kt == qt))
                last.then_inc(ctx_ready, 1)

            def turn_ctx(s, i, g, par):
                pe.wait_ge(ctx_normed, g + 1)
                b = fill_work(s, "ctxT", i)
                transposes(b, [ctxn[:, par, t].rearrange("p h d -> p (h d)") for t in range(BLOCK_TILES)])

            def project_out(s):
                b = fill_work(s, "proj")
                if isinstance(s, str):
                    drained(s, "ctxT", 2)
                else:
                    drained(s, "ctxT", 2)
                for c in range(C):
                    cols = slice(c * P, (c + 1) * P)
                    last = product3(ps_work[:, b, :], (w_hi[3][:, cols], w_lo[3][:, cols]),
                                    (cT_hi[:, c, :], cT_lo[:, c, :]), start=(c == 0), stop=(c == C - 1))
                last.then_inc(work_filled[b], 1)

            def turn_attn(s):
                drained(s, "proj")
                b = fill_work(s, "attn")
                transposes(b, [aT[:, t * P:(t + 1) * P] for t in range(BLOCK_TILES)])

            def turn_x1(s, blk):
                pe.wait_ge(x1_ready, blk + 1)
                b = fill_work(s, "x1T")
                transposes(b, [pay[:, t, 0:D] for t in range(BLOCK_TILES)])

            def affinities(s):
                drained(s, "x1T")
                b = fill_work(s, "aff")
                for t in range(BLOCK_TILES):
                    last = pe.matmul(ps_work[:, b, t * E:(t + 1) * E], x1T[:, t * P:(t + 1) * P], cenT[:],
                                     start=True, stop=True)
                last.then_inc(work_filled[b], 1)

            def ranks(s, blk):
                pe.wait_ge(chosen_ready, blk + 1)
                b = fill_work(s, "rank")
                o = ps_work[:, b, 0:BLOCK_TILES * E]
                pe.matmul(o, before[:], chosen[:].rearrange("p t e -> p (t e)"), start=True, stop=False)
                pe.matmul(o, ones[:], seen[:, 0:BLOCK_TILES, :].rearrange("p t e -> p (t e)"), start=False,
                          stop=True).then_inc(work_filled[b], 1)

            def body(s, first=False):
                for i in range(8):
                    if i == 0:
                        turn_x(s)
                    if i or not first:
                        scores(8 * s - 1 + i, (i + 1) % 2, s, i)
                    project_qk(s, i)
                    if i >= 2 or not first:
                        if i == 2:
                            pe.wait_ge(v_split, 8 * s + 4)
                        if i == 6:
                            pe.wait_ge(v_split, 8 * s + 8)
                        contexts(8 * s - 2 + i, i % 2, (i - 2) % 8)
                    if i == 3 and not first:
                        project_out(s)
                    if i >= 3 or not first:
                        turn_ctx(s, i, 8 * s - 3 + i, (i + 1) % 2)
                    if i == 1:
                        for u in range(4):
                            project_v(s, u)
                    if 2 <= i <= 5:
                        project_v(s, i + 2)
                    if not first:
                        if i == 4:
                            turn_attn(s)
                        if i == 5:
                            turn_x1(s, s - 1)
                        if i == 6:
                            affinities(s)
                        if i == 7:
                            ranks(s, s - 1)

            pe.wait_ge(pool_step, 4)
            pe.wait_ge(small_loaded, 16 * (N_SMALL + 1))
            pe.transpose(ps_ctx[:, 0, 0:P], small_rows[:], ident[:]).then_inc(small_turned, 1)
            pe.wait_ge(consts_ready, 2)
            body(0, True)
            pe.wait_ge(wproj_split, 5)
            with pe.Fori(1, BLOCKS) as s:
                body(s)

            def turn_weights(n):
                pe.wait_ge(exp_done, 16 * BLOCKS)
                if n >= 4:
                    pe.wait_ge(turn_drained, n - 3)
                for k in range(FK):
                    src = w1n[:, n * FK + k, :] if n < E else w2n[:, n - E, k * P:(k + 1) * P]
                    last = pe.transpose(ps_scores[:, n % 4, k * P:(k + 1) * P], src, ident[:])
                last.then_inc(turned, 1)

            scores(8 * BLOCKS - 1, 1, "tail", 0)
            contexts(8 * BLOCKS - 2, 0, C - 2)
            turn_ctx("tail", 0, 8 * BLOCKS - 3, 1)
            pe.wait_ge(wffn_loaded, 48)
            contexts(8 * BLOCKS - 1, 1, C - 1)
            turn_ctx("tail", 1, 8 * BLOCKS - 2, 0)
            for n in range(0, 4):
                turn_weights(n)
            turn_ctx("tail", 2, 8 * BLOCKS - 1, 1)
            for n in range(4, 8):
                turn_weights(n)
            project_out("tail")
            for n in range(8, 12):
                turn_weights(n)
            turn_attn("tail")
            for n in range(12, 16):
                turn_weights(n)
            turn_x1("tail", BLOCKS - 1)
            affinities("tail")
            ranks("tail", BLOCKS - 1)
            b = fill_work("tail", "count")
            pe.matmul(ps_work[:, b, 0:E], ones[:], seen[:, BLOCK_TILES, :], start=True, stop=True).then_inc(work_filled[b], 1)

            def turn_n(j):
                pe.wait_ge(nrm_ready, j + 1)
                if j >= 2:
                    pe.wait_ge(hin_ready, j - 1)
                pe.transpose(ps_work[:, j % 2, 0:P], nrm[:, j % 2, :], ident[:]).then_inc(nT_filled, 1)

            def up(j):
                pe.wait_ge(hin_ready, j + 1)
                if j >= 2:
                    pe.wait_ge(hT_ready, FK * (j - 1))
                for k in range(FK):
                    last = pe.matmul(ps_scores[:, j % 2, k * P:(k + 1) * P], wst[:, j % RING, k * P:(k + 1) * P],
                                     hin[:, j % 2, :], start=True, stop=True)
                last.then_inc(h_filled, 1)

            def down(j):
                e = pe.value_load(table[0:1, 0, j:j + 1], min_val=0, max_val=E - 1)
                pe.wait_ge(hT_ready, FK * (j + 1))
                if j >= 2:
                    pe.wait_ge(f_drained, j - 1)
                for k in range(FK):
                    last = pe.matmul(ps_scores[:, 2 + j % 2, 0:D], hT[:, j % 2, k * P:(k + 1) * P],
                                     w2T[:, bass.ds(e * F + k * P, D)], start=(k == 0), stop=(k == FK - 1))
                last.then_inc(f_filled, 1)

            pe.wait_ge(turn_drained, 2 * E)
            pe.wait_ge(table_ready, 1)
            for j in range(-1, TILES + 1):
                if j + 1 < TILES:
                    turn_n(j + 1)
                if 0 <= j < TILES:
                    up(j)
                if j >= 1:
                    down(j - 1)


_INS = ['L0_attn_states', 'L0_attn_Wq', 'L0_attn_bq', 'L0_attn_Wk', 'L0_attn_bk', 'L0_attn_Wv', 'L0_attn_bv',
        'L0_attn_Wo', 'L0_attn_bo', 'L0_ffn_centroids', 'L0_ffn_ln_g', 'L0_ffn_ln_b', 'L0_ffn_w1', 'L0_ffn_b1',
        'L0_ffn_w2', 'L0_ffn_b2']
_OUTS = [((8, 256, 128), 'float32')]


def kernel(**inputs):
    import numpy as _np
    import concourse.bacc as _bacc
    from concourse import mybir as _mybir
    from concourse.bass_utils import run_bass_kernel_spmd as _run

    nc = _bacc.Bacc("TRN2", target_bir_lowering=False, num_devices=1)
    arrays, args = {}, []
    for name in _INS:
        a = _np.ascontiguousarray(inputs[name])
        arrays[f"in_{name}_dram"] = a
        args.append(nc.dram_tensor(f"in_{name}_dram", a.shape, _mybir.dt.from_np(a.dtype), kind="ExternalInput").ap())
    for i, (shape, dtype) in enumerate(_OUTS):
        dt = _mybir.dt.from_np(_np.dtype(dtype))
        args.append(nc.dram_tensor(f"out_{i}_dram", shape, dt, kind="ExternalOutput").ap())
    attention_moe(nc, *args)
    r = _run(nc, [arrays], core_ids=[0])
    got = tuple(r.results[0][f"out_{i}_dram"] for i in range(len(_OUTS)))
    return got[0]
```

```python
import math
from contextlib import ExitStack

import concourse.bass as bass
from concourse import mybir
from concourse.alu_op_type import AluOpType as ALU

ACT = mybir.ActivationFunctionType
AX = mybir.AxisListType
F32 = mybir.dt.float32
F32R = mybir.dt.float32r
BF16 = mybir.dt.bfloat16
F16 = mybir.dt.float16
I32 = mybir.dt.int32
U32 = mybir.dt.uint32

P = 128
EPS = 1e-5
BLOCK_TILES = 4
BLOCK = BLOCK_TILES * P
PAD_TILES = 8
ROW = P + 4
ALPHA, TOKEN, MEAN, RSTD = P, P + 1, P + 2, P + 3
LOADS = 12
RING = 4


PROB_FACTOR = 16.0
VALUE_FACTOR = 4096.0


def work_plan(first):
    plan = []
    for i in range(8):
        if i == 0:
            plan.append(("xT", 0))
        if i == 6 and not first:
            plan.append(("x1T", 0))
        plan += [("q", i), ("k", i)]
        if i == 3 and not first:
            plan.append(("proj", 0))
        if i >= 3 or not first:
            plan.append(("ctxT", i))
        if i < 2:
            plan += [("v", 2 * i), ("v", 2 * i + 1)]
        if 2 <= i <= 5:
            plan.append(("v", i + 2))
        if not first:
            plan += {4: [("attn", 0)], 6: [("aff", 0)], 7: [("rank", 0)]}.get(i, [])
    return plan


TAIL_PLAN = [("ctxT", 0), ("proj", 0), ("ctxT", 1), ("ctxT", 2), ("attn", 0), ("x1T", 0), ("aff", 0),
             ("rank", 0), ("count", 0)]
WORK_BANKS = 3


def attention_moe(nc, x, Wq, bq, Wk, bk, Wv, bv, Wo, bo, cen, ln_g, ln_b, w1, b1, w2, b2, out):
    B, S, D = x.shape
    HD = Wq.shape[1]
    E, F, _ = w1.shape
    N = B * S
    DH = 64
    C = HD // P
    BLOCKS = N // BLOCK
    FK = F // P
    TILES = N // P + E - 1
    DV = DH + 1
    WBC = F + FK + 2
    SLOTS = E * N + PAD_TILES * P
    assert (S, D, DH * 2, C, BLOCK) == (2 * P, P, P, 8, 2 * S)

    slots = nc.dram_tensor("slots", [SLOTS, ROW], F32, kind="Internal").ap()
    x_rows = x.rearrange("b s d -> (b s) d")
    out_rows = out.rearrange("b s d -> (b s) d")

    with ExitStack() as ctx:
        def sb(name, shape, dt=F32):
            return ctx.enter_context(nc.sbuf_tensor(name, shape, dt))

        def sem(name):
            return ctx.enter_context(nc.semaphore(name))

        ps_scores = ctx.enter_context(nc.psum_tensor("ps_scores", [P, 3, 512], F32))
        ps_ctx = ctx.enter_context(nc.psum_tensor("ps_ctx", [P, 2, 512], F32))
        ps_work = ctx.enter_context(nc.psum_tensor("ps_work", [P, WORK_BANKS, 512], F32))
        ps_down = [ps_scores[:, 2, 0:D], ps_work[:, 2, 0:D]]

        ident = sb("ident", [P, P])
        seen_keys = sb("seen_keys", [P, P])
        before = sb("before", [P, P], BF16)
        ones = sb("ones", [P, P], BF16)
        ones_rows = sb("ones_rows", [64, P], F32R)
        region = sb("region", [P, E])
        expert_ids = sb("expert_ids", [P, E])
        thresholds = sb("thresholds", [P, 16])
        upto = sb("upto", [P, E, E])
        tile_ids = sb("tile_ids", [P, TILES])
        fill = sb("fill", [P, ROW])
        small_rows = sb("small_rows", [P, P])
        small = sb("small", [P, P])
        bv_parts = sb("bv_parts", [64, HD], F32R)
        b2_all = sb("b2_all", [P, E, D])
        x_in = sb("x_in", [P, BLOCK_TILES, D])
        x_res = sb("x_res", [P, BLOCK_TILES, D])
        xT_hi = sb("xT_hi", [P, BLOCK], F32R)
        xT_lo = sb("xT_lo", [P, BLOCK], F32R)
        w_hi = [sb(f"w_hi{n}", [P, HD], F32R) for n in range(4)]
        w_lo = [sb(f"w_lo{n}", [P, HD], F32R) for n in range(4)]
        w2T = sb("w2T", [P, E * F])
        qT, kT, v32 = (w2T[:, n * 2 * BLOCK:(n + 1) * 2 * BLOCK].rearrange("p (a c) -> p a c", a=2) for n in range(3))
        v_hi = sb("v_hi", [P, BLOCK_TILES, 2 * C, DV], F16)
        v_lo = sb("v_lo", [P, BLOCK_TILES, 2 * C, DH], F16)
        p_hi = sb("p_hi", [P, 2, 3 * BLOCK], F16)
        p_lo = sb("p_lo", [P, 2, 3 * BLOCK], F16)
        log_factor = sb("log_factor", [P, 1])
        probs = sb("probs", [P, 2, 3 * BLOCK])
        rden = sb("rden", [P, 2, BLOCK_TILES, 1])
        ctxn = sb("ctxn", [P, 2, BLOCK_TILES, 2, DH])
        cT_hi = sb("cT_hi", [P, C, BLOCK], F32R)
        cT_lo = sb("cT_lo", [P, C, BLOCK], F32R)
        aT = sb("aT", [P, BLOCK])
        bv_row = v32[0:1].rearrange("p a c -> p (a c)")
        y = sb("y", [P, BLOCK_TILES, D])
        stats = sb("stats", [P, BLOCK_TILES, 6])
        mv = sb("mv", [P, BLOCK_TILES, 2])
        var_eps = sb("var_eps", [P, BLOCK_TILES, 1])
        minus_half = sb("minus_half", [P, BLOCK_TILES, 1])
        rstd = sb("rstd", [P, BLOCK_TILES, 1])
        pay = sb("pay", [P, BLOCK_TILES, ROW])
        x1T = sb("x1T", [P, BLOCK])
        cenT = sb("cenT", [P, E])
        aff = sb("aff", [P, BLOCK_TILES, E])
        top = sb("top", [P, BLOCK_TILES, 8])
        top_at = sb("top_at", [P, BLOCK_TILES, 8], U32)
        top_f = sb("top_f", [P, BLOCK_TILES, 1])
        exp_neg = sb("exp_neg", [P, BLOCK_TILES, 1])
        exp_one = sb("exp_one", [P, BLOCK_TILES, 1])
        chosen = sb("chosen", [P, BLOCK_TILES, E], BF16)
        seen = sb("seen", [P, E], BF16)
        block_sum = sb("block_sum", [P, E, 1])
        slot8 = sb("slot8", [P, BLOCK_TILES, E])
        slot8c = sb("slot8c", [P, BLOCK_TILES, E])
        slot_f = sb("slot_f", [P, BLOCK_TILES, 1])
        slot_i = sb("slot_i", [P, BLOCK_TILES], U32)
        token_f = sb("token_f", [P, BLOCK_TILES, 1])
        w1n = sb("w1n", [P, E * FK, D])
        w2n = sb("w2n", [P, E, F])
        wb = sb("wb", [P, E * WBC])
        stage = wb[:, 0:4 * HD]
        n_e = sb("n_e", [P, E])
        over = sb("over", [P, E, 16])
        tiles_e = sb("tiles_e", [P, E])
        ends8 = sb("ends8", [P, E, E])
        ends = sb("ends", [P, E])
        past = sb("past", [P, TILES, E])
        past_t = sb("past_t", [P, TILES, E])
        exp_of = sb("exp_of", [P, TILES])
        skipped = sb("skipped", [P, TILES])
        row_of = sb("row_of", [P, TILES])
        row_of2 = sb("row_of2", [P, TILES])
        table = sb("table", [P, 2, -(-TILES // 4) * 4], I32)
        free = [w1n[:].rearrange("p n d -> p (n d)"), w2n[:].rearrange("p n d -> p (n d)")]
        taken = [0, 0]

        def over_weights(side, parts, width):
            at = taken[side]
            taken[side] += parts * width
            return free[side][:, at:taken[side]].rearrange("p (a d) -> p a d", a=parts)

        wst = over_weights(0, RING, WBC)
        xx = over_weights(0, RING, D)
        fin = over_weights(0, RING, D)
        xg = over_weights(1, LOADS, ROW)
        nrm = over_weights(1, 2, D)
        hin = over_weights(1, 2, P)
        hT = over_weights(1, 2, FK * P)
        fy = over_weights(1, 2, D)
        fz = over_weights(1, 2, D)
        sd3 = sb("sd3", [P, 2, 1])
        st3 = sb("st3", [P, 2, 6])
        mv3 = sb("mv3", [P, 2, 2])
        rs3 = sb("rs3", [P, 2, 1])
        eps = sb("eps", [P, 1])

        consts_ready = sem("consts_ready")
        memset_done = sem("memset_done")
        ident_ready = sem("ident_ready")
        w_hi_ready = sem("w_hi_ready")
        x_loaded = sem("x_loaded")
        xres_loaded = sem("xres_loaded")
        wproj_loaded = [sem(f"wproj_loaded{n}") for n in range(4)]
        qk_bias_loaded = sem("qk_bias_loaded")
        bv_loaded = sem("bv_loaded")
        bv_cleared = sem("bv_cleared")
        small_loaded = sem("small_loaded")
        wffn_loaded = sem("wffn_loaded")
        small_turned = sem("small_turned")
        small_ready = sem("small_ready")
        slots_filled = sem("slots_filled")
        wproj_split = sem("wproj_split")
        pool_step = sem("pool_step")
        dve_step = sem("dve_step")
        wait_taken = sem("wait_taken")
        work_filled = [sem(f"work_filled{b}") for b in range(WORK_BANKS)]
        work_drained = [sem(f"work_drained{b}") for b in range(WORK_BANKS)]
        scores_ready = sem("scores_ready")
        head_scored = sem("head_scored")
        exp_done = sem("exp_done")
        probs_masked = sem("probs_masked")
        p_hi_ready = sem("p_hi_ready")
        probs_ready = sem("probs_ready")
        v_split = sem("v_split")
        ctx_ready = sem("ctx_ready")
        ctx_normed = sem("ctx_normed")
        y_ready = sem("y_ready")
        var_ready = sem("var_ready")
        rstd_ready = sem("rstd_ready")
        mvout_ready = sem("mvout_ready")
        sdout_ready = sem("sdout_ready")
        x1_ready = sem("x1_ready")
        x1T_ready = sem("x1T_ready")
        top_ready = sem("top_ready")
        expneg_ready = sem("expneg_ready")
        chosen_ready = sem("chosen_ready")
        seen_ready = sem("seen_ready")
        slot_ready = sem("slot_ready")
        scatter_begun = sem("scatter_begun")
        scattered = sem("scattered")
        turned = sem("turned")
        turn_drained = sem("turn_drained")
        table_ready = sem("table_ready")
        slots_loaded = [sem(f"slots_loaded{n}") for n in range(LOADS)]
        wst_loaded = [sem(f"wst_loaded{n}") for n in range(RING)]
        fz_ready = sem("fz_ready")
        st3_ready = sem("st3_ready")
        rs3_ready = sem("rs3_ready")
        nrm_ready = sem("nrm_ready")
        twice_ready = sem("twice_ready")
        nT_filled = sem("nT_filled")
        hin_ready = sem("hin_ready")
        h_filled = sem("h_filled")
        hT_ready = sem("hT_ready")
        f_filled = sem("f_filled")
        f_drained = sem("f_drained")
        fin_ready = sem("fin_ready")
        stored = [sem(f"stored{n}") for n in range(LOADS)]

        first_plan, steady_plan = work_plan(True), work_plan(False)

        def work(s, kind, i=0):
            plan = TAIL_PLAN if isinstance(s, str) else first_plan if isinstance(s, int) and s == 0 else steady_plan
            k = plan.index((kind, i))
            bank = bank_of(plan, k)
            n = sum(bank_of(plan, j) == bank for j in range(k + 1))
            if plan is not first_plan:
                n = n + bank_uses(first_plan, bank)
            if plan is steady_plan:
                n = n + (s - 1) * bank_uses(steady_plan, bank)
            if plan is TAIL_PLAN:
                n = n + (BLOCKS - 1) * bank_uses(steady_plan, bank)
            return bank, n

        def bank_of(plan, k):
            return (k - (plan.index(("k", 7)) if plan is not TAIL_PLAN else -1)) % WORK_BANKS

        def bank_uses(plan, bank):
            return sum(bank_of(plan, j) == bank for j in range(len(plan)))

        def last_keys(s):
            for plan in (first_plan, steady_plan):
                assert [bank_of(plan, j) for j in range(plan.index(("k", 7)), len(plan))].count(0) == 1
            return 0, bank_uses(first_plan, 0) + (s - 1) * bank_uses(steady_plan, 0)

        def wait(eng, s, value):
            if isinstance(value, int) and value <= 0:
                return
            eng.wait_ge(s, value)

        def table_row(n, engine, most):
            _, values = nc.values_load_multi_w_load_instructions(
                table[0:1, n, 0:TILES], engines=(engine,), min_val=0, max_val=most,
                skip_runtime_bounds_check_because="the table's values are clamped to the experts' and slots' ranges")
            return values

        BQ, BK, BO, B1, LG, LB, CEN = 0, C, 2 * C, 2 * C + 1, 2 * C + 1 + E * FK, 2 * C + 1 + E * FK + E, 2 * C + 1 + E * FK + 2 * E
        SMALL = CEN + E
        N_SMALL = 5

        BODY_LINKS = 35

        block = ctx.enter_context(nc.Block())

        @block.sync
        def _(sp):
            def x_tiles(s):
                return x_rows[bass.ds(s * BLOCK, BLOCK), :].rearrange("(t p) d -> p t d", p=P)

            sp.dma_start(x_in[:], x_tiles(0)).then_inc(x_loaded, 16)
            for n, w in enumerate((Wq, Wk, Wv)):
                sp.dma_start(stage[:, n * HD:(n + 1) * HD], w).then_inc(wproj_loaded[n], 16)
                if n == 0:
                    sp.dma_start(bv_row, bv.rearrange("(o n) -> o n", o=1)).then_inc(bv_loaded, 16)
            sp.dma_start(stage[:, 3 * HD:4 * HD].rearrange("p (c d) -> p c d", c=C),
                         Wo.rearrange("(c p) d -> p c d", p=P)).then_inc(wproj_loaded[3], 16)
            sp.wait_ge(exp_done, 2)
            sp.dma_start(w1n[:].rearrange("p (e k) d -> p e k d", e=E),
                         w1.rearrange("e (k p) d -> p e k d", p=P)).then_inc(wffn_loaded, 16)
            sp.dma_start(w2n[:], w2.rearrange("e d f -> d e f")).then_inc(wffn_loaded, 16)
            sp.dma_start(b2_all[:].rearrange("p e d -> p (e d)"),
                         b2.rearrange("e d -> (e d)").partition_broadcast(P)).then_inc(wffn_loaded, 16)
            sp.wait_ge(consts_ready, 1)
            tiles = SLOTS // P
            per = tiles // 4
            view = slots.rearrange("(n p) c -> p n c", p=P)
            for n in range(4):
                sp.dma_start(view[:, n * per:(n + 1) * per, :],
                             fill[:].unsqueeze(1).broadcast_to([P, per, ROW])).then_inc(slots_filled, 16)

            def body(s):
                b, n = work(s - 1, "xT")
                sp.wait_ge(work_drained[b], n)
                sp.dma_start(x_in[:], x_tiles(s)).then_inc(x_loaded, 16)
                wait(sp, y_ready, s - 1)
                sp.dma_start(x_res[:], x_tiles(s - 1)).then_inc(xres_loaded, 16)

            body(1)
            with sp.Fori(2, BLOCKS) as s:
                body(s)
            sp.wait_ge(y_ready, BLOCKS - 1)
            sp.dma_start(x_res[:], x_tiles(BLOCKS - 1)).then_inc(xres_loaded, 16)

            sp.wait_ge(table_ready, 1)
            experts = table_row(0, mybir.EngineType.SP, E - 1)
            rows = table_row(1, mybir.EngineType.SP, SLOTS - P)

            def load_weights(j):
                if j >= RING:
                    sp.wait_ge(hT_ready, FK * (j - RING + 1))
                sp.dma_start(wst[:, j % RING, :], wb[:, bass.ds(experts[j] * WBC, WBC)]).then_inc(wst_loaded[j % RING], 16)

            def load_rows(j):
                if j >= LOADS:
                    sp.wait_ge(stored[j % LOADS], 16 * (j // LOADS))
                sp.dma_start(xg[:, j % LOADS, :], slots[bass.ds(rows[j], P), :]).then_inc(slots_loaded[j % LOADS], 16)

            sp.wait_ge(turn_drained, 2 * E)
            load_weights(0)
            load_weights(1)
            sp.wait_ge(scattered, 16 * BLOCKS * BLOCK_TILES)
            for j in range(RING):
                load_rows(j)
            for j in range(2, TILES):
                load_weights(j)
                if j + 2 < TILES:
                    load_rows(j + 2)

        @block.gpsimd
        def _(pool):
            count = [0]

            def link(ins):
                count[0] += 1
                ins.then_inc(pool_step, 1)
                pool.wait_ge(pool_step, count[0])

            pool.memset(small_rows[:], 0.0).then_inc(memset_done, 1)
            link(pool.memset(ident[:], 0.0))
            pool.affine_select(out=ident[:], in_=ident[:], compare_op=ALU.not_equal, fill=1.0, base=0,
                               pattern=[[-1, P]], channel_multiplier=1).then_inc(ident_ready, 1)
            pool.memset(bv_parts[:].bitcast(F32), 0.0).then_inc(bv_cleared, 1)
            link(pool.memset(fill[:], 0.0))
            link(pool.iota(fill[:].bitcast(I32)[:, TOKEN:TOKEN + 1], pattern=[[0, 1]], base=N, channel_multiplier=1))
            pool.nop().then_inc(consts_ready, 1)
            link(pool.memset(ones[:], 1.0))
            link(pool.affine_select(out=before[:], in_=ones[:], compare_op=ALU.is_gt, fill=0.0, base=0,
                                    pattern=[[1, P]], channel_multiplier=-1))
            link(pool.memset(seen_keys[:], 1.0))
            link(pool.affine_select(out=seen_keys[:], in_=seen_keys[:], compare_op=ALU.is_ge, fill=0.0, base=0,
                                    pattern=[[1, P]], channel_multiplier=-1))
            pool.iota(region[:], pattern=[[N, E]], base=0, channel_multiplier=0, allow_small_or_imprecise_dtypes=True)
            pool.iota(expert_ids[:], pattern=[[1, E]], base=0, channel_multiplier=0, allow_small_or_imprecise_dtypes=True)
            pool.iota(thresholds[:], pattern=[[P, 16]], base=0, channel_multiplier=0, allow_small_or_imprecise_dtypes=True)
            pool.iota(tile_ids[:], pattern=[[1, TILES]], base=0, channel_multiplier=0, allow_small_or_imprecise_dtypes=True)
            pool.iota(token_f[:], pattern=[[P, BLOCK_TILES]], base=0, channel_multiplier=1, allow_small_or_imprecise_dtypes=True)
            link(pool.memset(upto[:], 1.0))
            link(pool.affine_select(out=upto[:], in_=upto[:], compare_op=ALU.is_ge, fill=0.0, base=0,
                                    pattern=[[1, E], [-1, E]], channel_multiplier=0))
            link(pool.memset(v_hi[:, :, :, DH:DV], VALUE_FACTOR))
            link(pool.memset(log_factor[:], math.log(PROB_FACTOR)))
            link(pool.memset(pay[:], 0.0))
            link(pool.memset(minus_half[:], -0.5))
            link(pool.memset(eps[:], EPS))
            link(pool.memset(ones_rows[:].bitcast(F32), 1.0))
            pool.nop().then_inc(consts_ready, 1)

            def mask(g, par):
                for part, (start, end, step) in enumerate(((0, 2 * BLOCK, S), (2 * BLOCK, 3 * BLOCK, P))):
                    pool.wait_ge(exp_done, 2 * g + part + 1)
                    v = probs[:, par, start:end].rearrange("p (n q) -> p n q", q=step)[:, :, 0:P]
                    pool.tensor_tensor(v, v, seen_keys[:].unsqueeze(1).broadcast_to([P, 4, P]),
                                       ALU.mult).then_inc(probs_masked, 1)

            def root(b, inner):
                pool.wait_ge(var_ready, 2 * b + inner + 1)
                pool.tensor_tensor(pay[:, :, RSTD:RSTD + 1] if inner else rstd[:], var_eps[:], minus_half[:],
                                   ALU.pow).then_inc(rstd_ready, 1)

            def scatter(b):
                pool.wait_ge(slot_ready, b + 1)
                pool.sem_inc(scatter_begun, 1)
                for t in range(BLOCK_TILES):
                    pool.indirect_dma_start(slots, bass.IndirectOffsetOnAxis(ap=slot_i[:, t:t + 1], axis=0),
                                            pay[:, t, :], None, bounds_check=SLOTS - 1,
                                            oob_is_err=False).then_inc(scattered, 16)

            def body(s, steady=True):
                first = isinstance(s, int) and s == 0
                for i in range(8):
                    if i or not first:
                        mask(8 * s - 1 + i, (i + 1) % 2)
                    if i == 1 and steady:
                        root(s - 2, 1)
                    if i == 2 and steady:
                        scatter(s - 2)
                    if i == 4 and not first:
                        root(s - 1, 0)

            body(0, False)
            body(1, False)
            pool.wait_ge(slots_filled, 64)
            with pool.Fori(2, BLOCKS) as s:
                body(s)
            mask(8 * BLOCKS - 1, 1)
            root(BLOCKS - 2, 1)
            scatter(BLOCKS - 2)
            root(BLOCKS - 1, 0)
            root(BLOCKS - 1, 1)
            scatter(BLOCKS - 1)

            for j in range(TILES):
                pool.wait_ge(fin_ready, j + 1)
                pool.indirect_dma_start(out_rows, bass.IndirectOffsetOnAxis(
                    ap=xg.bitcast(U32)[:, j % LOADS, TOKEN:TOKEN + 1], axis=0), fin[:, j % RING, :], None,
                    bounds_check=N - 1, oob_is_err=False).then_inc(stored[j % LOADS], 16)
            for q in range(LOADS):
                pool.wait_ge(stored[q], 16 * len(range(q, TILES, LOADS)))

        @block.scalar
        def _(act):
            def tanh_qk(s, i):
                par = i % 2
                for kind, dst, base in (("q", qT, BQ), ("k", kT, BK)):
                    b, n = work(s, kind, i)
                    act.wait_ge(work_filled[b], n)
                    act.activation(dst[:, par, :], ps_work[:, b, :], ACT.Tanh,
                                   bias=small[:, base + i:base + i + 1]).then_inc(work_drained[b], 1)

            def tanh_v(s, u):
                b, n = work(s, "v", u)
                act.wait_ge(work_filled[b], n)
                wait(act, v_split, 8 * s + u - 1)
                act.activation(v32[:, u % 2, :], ps_work[:, b, :], ACT.Tanh).then_inc(work_drained[b], 1)

            def high_probs(g, par):
                for part, cols in enumerate((slice(0, 2 * BLOCK), slice(2 * BLOCK, 3 * BLOCK))):
                    act.wait_ge(probs_masked, 2 * g + part + 1)
                    act.copy(p_hi[:, par, cols], probs[:, par, cols]).then_inc(p_hi_ready, 1)

            def exp_scores(g, par):
                act.wait_ge(scores_ready, g + 1)
                ps = ps_scores[:].rearrange("p b c -> p (b c)")
                for cols in (slice(0, 2 * BLOCK), slice(2 * BLOCK, 3 * BLOCK)):
                    act.activation(probs[:, par, cols], ps[:, cols], ACT.Exp, scale=DH ** -0.5,
                                   bias=log_factor[:]).then_inc(exp_done, 1)

            def tanh_out(s):
                b, n = work(s, "proj")
                act.wait_ge(work_filled[b], n)
                act.activation(aT[:], ps_work[:, b, :], ACT.Tanh, bias=small[:, BO:BO + 1]).then_inc(work_drained[b], 1)

            def copy_x1T(s):
                b, n = work(s, "x1T")
                act.wait_ge(work_filled[b], n)
                act.copy(x1T[:], ps_work[:, b, :]).then_inc(work_drained[b], 1)

            def exp_gate(blk):
                act.wait_ge(top_ready, blk + 1)
                act.activation(exp_neg[:], top[:, :, 0:1], ACT.Exp, scale=-1.0).then_inc(expneg_ready, 1)

            def body(s, first=False):
                for i in range(8):
                    if i or not first:
                        exp_scores(8 * s - 1 + i, (i + 1) % 2)
                    if i == 6 and not first:
                        copy_x1T(s)
                    tanh_qk(s, i)
                    if i == 0 and first:
                        act.wait_ge(small_turned, 2)
                        act.copy(small[:, 2 * C:SMALL], ps_ctx[:, 1, 2 * C:SMALL]).then_inc(small_ready, 1)
                        act.wait_ge(small_ready, 2)
                    if i == 3 and not first:
                        tanh_out(s)
                    if i or not first:
                        high_probs(8 * s - 1 + i, (i + 1) % 2)
                    if i < 2:
                        tanh_v(s, 2 * i)
                        tanh_v(s, 2 * i + 1)
                    if 2 <= i <= 5:
                        tanh_v(s, i + 2)
                    if i == 7 and not first:
                        exp_gate(s - 1)

            act.wait_ge(memset_done, 1)
            act.dma_start(small_rows[BQ:BQ + C, :], bq.rearrange("(c p) -> c p", p=P)).then_inc(qk_bias_loaded, 16)
            act.dma_start(small_rows[BK:BK + C, :], bk.rearrange("(c p) -> c p", p=P)).then_inc(qk_bias_loaded, 16)
            for n in range(2):
                act.wait_ge(wproj_loaded[n], 16)
                act.copy(w_hi[n][:], stage[:, n * HD:(n + 1) * HD]).then_inc(w_hi_ready, 1)
            for row, n, src in ((BO, 1, bo.rearrange("(c p) -> c p", p=P)), (B1, E * FK, b1.rearrange("e (k p) -> (e k) p", p=P)),
                                (LG, E, ln_g), (LB, E, ln_b), (CEN, E, cen)):
                act.dma_start(small_rows[row:row + n, :], src).then_inc(small_loaded, 16)
            act.wait_ge(small_turned, 1)
            act.copy(small[:, 0:2 * C], ps_ctx[:, 0, 0:2 * C]).then_inc(small_ready, 1)
            act.wait_ge(wproj_loaded[2], 16)
            act.copy(w_hi[2][:], stage[:, 2 * HD:3 * HD]).then_inc(w_hi_ready, 1)
            act.wait_ge(small_ready, 1)
            act.wait_ge(consts_ready, 2)
            body(0, True)
            with act.Fori(1, BLOCKS) as s:
                body(s)
            exp_scores(8 * BLOCKS - 1, 1)
            high_probs(8 * BLOCKS - 1, 1)

            wbv = wb[:].rearrange("p (e c) -> p e c", e=E)

            def drain_turned(n):
                act.wait_ge(turned, n + 1)
                dst = wbv[:, n, 0:F] if n < E else w2T[:, (n - E) * F:(n - E + 1) * F]
                act.copy(dst, ps_scores[:, n % 3, :]).then_inc(turn_drained, 1)

            for n in range(5):
                drain_turned(n)
            tanh_out("tail")
            for n in range(5, 11):
                drain_turned(n)
            copy_x1T("tail")
            for n in range(11, 16):
                drain_turned(n)
            exp_gate(BLOCKS - 1)

            def relu(j):
                act.wait_ge(h_filled, j + 1)
                for k in range(FK):
                    act.activation(hT[:, j % 2, k * P:(k + 1) * P], ps_scores[:, j % 2, k * P:(k + 1) * P], ACT.Relu,
                                   bias=wst[:, j % RING, F + k:F + k + 1]).then_inc(hT_ready, 1)

            def twice(j):
                act.wait_ge(slots_loaded[j % LOADS], 16 * (j // LOADS + 1))
                act.mul(xx[:, j % RING, :], xg[:, j % LOADS, 0:D], 2.0).then_inc(twice_ready, 1)

            def deviation(j):
                act.wait_ge(mvout_ready, j + 1)
                act.activation(sd3[:, j % 2, :], mv3[:, j % 2, 1:2], ACT.Sqrt, bias=eps[:]).then_inc(sdout_ready, 1)

            for j in range(TILES + 3):
                if j < TILES:
                    relu(j)
                    twice(j)
                if 2 <= j < TILES + 2:
                    deviation(j - 2)

        @block.vector
        def _(dve):
            before_piece, in_piece = [0], [0]

            def link(ins):
                in_piece[0] += 1
                ins.then_inc(dve_step, 1)
                dve.wait_ge(dve_step, before_piece[0] + in_piece[0])

            def low_weights(n):
                dve.wait_ge(w_hi_ready, n + 1)
                dve.tensor_tensor(w_lo[n][:], stage[:, n * HD:(n + 1) * HD], w_hi[n][:],
                                  ALU.subtract).then_inc(wproj_split, 1)

            def split_xT(s):
                b, n = work(s, "xT")
                dve.wait_ge(work_filled[b], n)
                link(dve.tensor_copy(xT_hi[:], ps_work[:, b, :]))
                dve.tensor_tensor(xT_lo[:], ps_work[:, b, :], xT_hi[:], ALU.subtract).then_inc(work_drained[b], 1)

            def normalise(g, par):
                dve.wait_ge(ctx_ready, g + 1)
                c = ps_ctx[:, :, 0:BLOCK_TILES * DV].rearrange("p h (t e) -> p h t e", e=DV)
                link(dve.reciprocal(rden[:], c[:, :, :, DH:DV]))
                dve.tensor_tensor(ctxn[:, par].rearrange("p t h d -> p h t d"), c[:, :, :, 0:DH],
                                  rden[:].broadcast_to([P, 2, BLOCK_TILES, DH]), ALU.mult).then_inc(ctx_normed, 1)

            def low_probs(g, par):
                for part, cols in enumerate((slice(0, 2 * BLOCK), slice(2 * BLOCK, 3 * BLOCK))):
                    dve.wait_ge(p_hi_ready, 2 * g + part + 1)
                    dve.tensor_tensor(p_lo[:, par, cols], probs[:, par, cols], p_hi[:, par, cols],
                                      ALU.subtract).then_inc(probs_ready, 1)

            def split_v(s, u):
                b, n = work(s, "v", u)
                t, heads = u % 4, slice(u // 4 * C, (u // 4 + 1) * C)
                dve.wait_ge(work_drained[b], n)
                src, hi = v32[:, u % 2, :].rearrange("p (h d) -> p h d", d=DH), v_hi[:, t, heads, 0:DH]
                link(dve.tensor_scalar(hi, src, VALUE_FACTOR, None, ALU.mult))
                dve.scalar_tensor_tensor(out=v_lo[:, t, heads, :], in0=src, scalar=VALUE_FACTOR, in1=hi,
                                         op0=ALU.mult, op1=ALU.subtract).then_inc(v_split, 1)

            def split_cT(s, i, c):
                b, n = work(s, "ctxT", i)
                dve.wait_ge(work_filled[b], n)
                link(dve.tensor_copy(cT_hi[:, c, :], ps_work[:, b, :]))
                dve.tensor_tensor(cT_lo[:, c, :], ps_work[:, b, :], cT_hi[:, c, :], ALU.subtract).then_inc(work_drained[b], 1)

            def residual_1(s, blk):
                b, n = work(s, "attn")
                dve.wait_ge(work_filled[b], n)
                dve.wait_ge(xres_loaded, 16 * (blk + 1))
                dve.tensor_tensor(y[:].rearrange("p t d -> p (t d)"), ps_work[:, b, :],
                                  x_res[:].rearrange("p t d -> p (t d)"), ALU.add).then_inc(work_drained[b], 1)
                dve.wait_ge(work_drained[b], n)
                for t in range(BLOCK_TILES):
                    last = dve.bn_stats(stats[:, t, :], y[:, t, :])
                link(last)
                dve.sem_inc(y_ready, 1)
                for t in range(BLOCK_TILES):
                    last = dve.bn_aggr(mv[:, t, :], stats[:, t, :])
                link(last)
                dve.tensor_scalar(var_eps[:], mv[:, :, 1:2], EPS, None, ALU.add).then_inc(var_ready, 1)

            def layer_norm_1(blk):
                dve.wait_ge(rstd_ready, 2 * blk + 1)
                wait(dve, scattered, 16 * BLOCK_TILES * blk)
                for t in range(BLOCK_TILES):
                    last = dve.tensor_scalar(pay[:, t, 0:D], y[:, t, :], mv[:, t, 0:1], rstd[:, t, :],
                                             ALU.subtract, ALU.mult)
                last.then_inc(x1_ready, 1)

            def inner_stats(blk):
                dve.wait_ge(x1_ready, blk + 1)
                for t in range(BLOCK_TILES):
                    last = dve.bn_stats(stats[:, t, :], pay[:, t, 0:D])
                link(last)
                dve.sem_inc(wait_taken, 1)
                for t in range(BLOCK_TILES):
                    last = dve.bn_aggr(mv[:, t, :], stats[:, t, :])
                link(last)
                dve.tensor_copy(pay[:, :, MEAN:MEAN + 1], mv[:, :, 0:1])
                dve.tensor_scalar(var_eps[:], mv[:, :, 1:2], EPS, None, ALU.add).then_inc(var_ready, 1)

            def choose(s, blk):
                b, n = work(s, "aff")
                dve.wait_ge(work_filled[b], n)
                dve.tensor_copy(aff[:].rearrange("p t e -> p (t e)"),
                                ps_work[:, b, 0:BLOCK_TILES * E]).then_inc(work_drained[b], 1)
                dve.wait_ge(work_drained[b], n)
                dve.sem_inc(wait_taken, 1)
                for t in range(BLOCK_TILES):
                    last = dve.max(top[:, t, :], aff[:, t, :])
                last.then_inc(top_ready, 1)
                dve.wait_ge(top_ready, blk + 1)
                dve.sem_inc(wait_taken, 1)
                for t in range(BLOCK_TILES):
                    last = dve.max_index(top_at[:, t, :], top[:, t, :], aff[:, t, :])
                link(last)
                link(dve.tensor_copy(top_f[:], top_at[:, :, 0:1]))
                dve.tensor_tensor(chosen[:], expert_ids[:].unsqueeze(1).broadcast_to([P, BLOCK_TILES, E]),
                                  top_f[:].broadcast_to([P, BLOCK_TILES, E]), ALU.is_equal).then_inc(chosen_ready, 1)

            def take_ranks(s):
                b, n = work(s, "rank")
                dve.wait_ge(work_filled[b], n)
                dve.tensor_tensor(slot8[:], ps_work[:, b, 0:BLOCK_TILES * E].rearrange("p (t e) -> p t e", e=E),
                                  region[:].unsqueeze(1).broadcast_to([P, BLOCK_TILES, E]),
                                  ALU.add).then_inc(work_drained[b], 1)

            def place(s, blk):
                dve.wait_ge(rstd_ready, 2 * blk + 2)
                dve.wait_ge(expneg_ready, blk + 1)
                link(dve.tensor_scalar(exp_one[:], exp_neg[:], 1.0, None, ALU.add))
                dve.reciprocal(pay[:, :, ALPHA:ALPHA + 1], exp_one[:])
                dve.tensor_copy(pay[:].bitcast(I32)[:, :, TOKEN:TOKEN + 1], token_f[:])
                b, n = work(s, "rank")
                dve.wait_ge(work_drained[b], n)
                link(dve.tensor_tensor(slot8c[:], slot8[:], chosen[:], ALU.mult))
                link(dve.tensor_reduce(slot_f[:], slot8c[:], AX.X, ALU.add))
                dve.tensor_copy(slot_i[:].unsqueeze(2), slot_f[:]).then_inc(slot_ready, 1)
                dve.tensor_scalar(token_f[:], token_f[:], float(BLOCK), None, ALU.add)
                if not isinstance(s, str):
                    link(dve.tensor_reduce(block_sum[:], chosen[:].rearrange("p t e -> p e t"), AX.X, ALU.add))
                    dve.tensor_tensor(seen[:].unsqueeze(2), seen[:].unsqueeze(2), block_sum[:], ALU.add).then_inc(seen_ready, 1)

            def body(s, first=False, steady=True):
                for i in range(8):
                    if i == 0:
                        if first:
                            dve.wait_ge(bv_cleared, 1)
                            dve.wait_ge(bv_loaded, 16)
                            link(dve.tensor_copy(bv_parts[0:1, :], bv_row))
                            dve.tensor_tensor(bv_parts[32:33, :], bv_row, bv_parts[0:1, :],
                                              ALU.subtract).then_inc(wproj_split, 1)
                            low_weights(0)
                        split_xT(s)
                        if steady:
                            take_ranks(s - 1)
                    if i == 0 and first:
                        low_weights(1)
                        low_weights(2)
                    if i == 2 and first:
                        dve.wait_ge(wproj_loaded[3], 16)
                        src = stage[:, 3 * HD:4 * HD]
                        link(dve.tensor_copy(w_hi[3][:], src))
                        dve.tensor_tensor(w_lo[3][:], src, w_hi[3][:], ALU.subtract).then_inc(wproj_split, 1)
                        dve.wait_ge(small_ready, 2)
                        dve.tensor_copy(cenT[:], small[:, CEN:CEN + E])
                        dve.memset(seen[:], 0.0).then_inc(seen_ready, 1)
                    if i >= 2 or not first:
                        normalise(8 * s - 2 + i, i % 2)
                    if i >= 3 or not first:
                        split_cT(s, i, (i + 5) % 8)
                    if i == 5 and not first:
                        layer_norm_1(s - 1)
                    if i or not first:
                        low_probs(8 * s - 1 + i, (i + 1) % 2)
                    if i < 2:
                        split_v(s, 2 * i)
                        split_v(s, 2 * i + 1)
                    if 2 <= i <= 5:
                        split_v(s, i + 2)
                    if not first:
                        if i == 4:
                            residual_1(s, s - 1)
                        if i == 6:
                            choose(s, s - 1)
                    if i == 0 and steady:
                        inner_stats(s - 2)
                    if i == 1 and steady:
                        place(s - 1, s - 2)

            body(0, first=True, steady=False)
            body(1, steady=False)
            before_loop = in_piece[0]
            with dve.Fori(2, BLOCKS) as s:
                before_piece[0], in_piece[0] = before_loop + (s - 2) * BODY_LINKS, 0
                body(s)
                assert in_piece[0] == BODY_LINKS, in_piece[0]
            before_piece[0], in_piece[0] = before_loop + (BLOCKS - 2) * BODY_LINKS, 0
            take_ranks(BLOCKS - 1)
            normalise(8 * BLOCKS - 2, 0)
            split_cT("tail", 0, C - 3)
            inner_stats(BLOCKS - 2)
            low_probs(8 * BLOCKS - 1, 1)
            split_cT("tail", 1, C - 2)
            normalise(8 * BLOCKS - 1, 1)
            place(BLOCKS - 1, BLOCKS - 2)
            split_cT("tail", 2, C - 1)
            wbv = wb[:].rearrange("p (e c) -> p e c", e=E)
            dve.tensor_copy(wbv[:, :, F:F + FK], small[:, B1:B1 + E * FK].rearrange("p (e k) -> p e k", e=E))
            dve.tensor_copy(wbv[:, :, F + FK:F + FK + 1], small[:, LG:LG + E].unsqueeze(2))
            dve.tensor_copy(wbv[:, :, F + FK + 1:F + FK + 2], small[:, LB:LB + E].unsqueeze(2))
            residual_1("tail", BLOCKS - 1)
            layer_norm_1(BLOCKS - 1)
            inner_stats(BLOCKS - 1)
            choose("tail", BLOCKS - 1)
            take_ranks("tail")
            place("tail", BLOCKS - 1)

            b, n = work("tail", "count")
            dve.wait_ge(work_filled[b], n)
            link(dve.tensor_copy(n_e[:], ps_work[:, b, 0:E]))
            link(dve.tensor_tensor(over[:], n_e[:].unsqueeze(2).broadcast_to([P, E, 16]),
                                   thresholds[:].unsqueeze(1).broadcast_to([P, E, 16]), ALU.is_gt))
            link(dve.tensor_reduce(tiles_e[:].unsqueeze(2), over[:], AX.X, ALU.add))
            link(dve.tensor_tensor(ends8[:], upto[:], tiles_e[:].unsqueeze(1).broadcast_to([P, E, E]), ALU.mult))
            link(dve.tensor_reduce(ends[:].unsqueeze(2), ends8[:], AX.X, ALU.add))
            link(dve.tensor_tensor(past[:], tile_ids[:].unsqueeze(2).broadcast_to([P, TILES, E]),
                                   ends[:].unsqueeze(1).broadcast_to([P, TILES, E]), ALU.is_ge))
            dve.tensor_reduce(exp_of[:].unsqueeze(2), past[:], AX.X, ALU.add)
            link(dve.tensor_tensor(past_t[:], past[:], tiles_e[:].unsqueeze(1).broadcast_to([P, TILES, E]), ALU.mult))
            link(dve.tensor_reduce(skipped[:].unsqueeze(2), past_t[:], AX.X, ALU.add))
            link(dve.tensor_tensor(row_of[:], tile_ids[:], skipped[:], ALU.subtract))
            link(dve.tensor_scalar(row_of2[:], row_of[:], float(P), None, ALU.mult))
            dve.tensor_scalar(table[:, 0, 0:TILES], exp_of[:], float(E - 1), None, ALU.min)
            link(dve.scalar_tensor_tensor(out=table[:, 1, 0:TILES], in0=exp_of[:], scalar=float(N), in1=row_of2[:],
                                          op0=ALU.mult, op1=ALU.add))
            dve.sem_inc(table_ready, 1)

            def norm_in(j):
                q = j % LOADS
                dve.wait_ge(slots_loaded[q], 16 * (j // LOADS + 1))
                dve.tensor_scalar(nrm[:, j % 2, :], xg[:, q, 0:D], xg[:, q, MEAN:MEAN + 1], xg[:, q, RSTD:RSTD + 1],
                                  ALU.subtract, ALU.mult).then_inc(nrm_ready, 1)

            def scale_in(j):
                p, w = j % 2, wst[:, j % RING, :]
                dve.wait_ge(nT_filled, j + 1)
                dve.wait_ge(wst_loaded[j % RING], 16 * (j // RING + 1))
                dve.tensor_scalar(hin[:, p, :], ps_work[:, p, 0:P], w[:, F + FK:F + FK + 1],
                                  w[:, F + FK + 1:F + FK + 2], ALU.mult, ALU.add).then_inc(hin_ready, 1)

            dve.wait_ge(table_ready, 1)
            experts = table_row(0, mybir.EngineType.DVE, E - 1)

            def add_b2(j):
                e = experts[j]
                dve.wait_ge(f_filled, j + 1)
                dve.tensor_tensor(fy[:, j % 2, :], ps_down[j % 2],
                                  b2_all[:].rearrange("p e d -> p (e d)")[:, bass.ds(e * D, D)],
                                  ALU.add).then_inc(f_drained, 1)

            def residual(j):
                dve.wait_ge(f_drained, j + 1)
                dve.wait_ge(twice_ready, j + 1)
                dve.scalar_tensor_tensor(out=fz[:, j % 2, :], in0=fy[:, j % 2, :],
                                         scalar=xg[:, j % LOADS, ALPHA:ALPHA + 1], in1=xx[:, j % RING, :],
                                         op0=ALU.mult, op1=ALU.add).then_inc(fz_ready, 1)

            def stats_out(j):
                dve.wait_ge(fz_ready, j + 1)
                dve.bn_stats(st3[:, j % 2, :], fz[:, j % 2, :]).then_inc(st3_ready, 1)

            def moments_out(j):
                dve.wait_ge(st3_ready, j + 1)
                dve.bn_aggr(mv3[:, j % 2, :], st3[:, j % 2, :]).then_inc(mvout_ready, 1)

            def inverse_out(j):
                dve.wait_ge(sdout_ready, j + 1)
                dve.reciprocal(rs3[:, j % 2, :], sd3[:, j % 2, :]).then_inc(rs3_ready, 1)

            def norm_out(j):
                p = j % 2
                dve.wait_ge(rs3_ready, j + 1)
                if j >= RING:
                    dve.wait_ge(stored[(j - RING) % LOADS], 16 * ((j - RING) // LOADS + 1))
                dve.tensor_scalar(fin[:, j % RING, :], fz[:, p, :], mv3[:, p, 0:1], rs3[:, p, :], ALU.subtract,
                                  ALU.mult).then_inc(fin_ready, 1)

            for j in range(-2, TILES + 3):
                for stage_of, at in ((scale_in, j + 1), (norm_in, j + 2), (add_b2, j - 2), (inverse_out, j - 3),
                                     (residual, j - 2), (norm_out, j - 3), (stats_out, j - 2), (moments_out, j - 2)):
                    if 0 <= at < TILES:
                        stage_of(at)

        @block.tensor
        def _(pe):
            def fill_work(s, kind, i=0):
                b, n = work(s, kind, i)
                wait(pe, work_drained[b], n - 1)
                return b

            def transposes(b, tiles):
                for t in range(BLOCK_TILES):
                    last = pe.transpose(ps_work[:, b, t * P:(t + 1) * P], tiles[t], ident[:])
                last.then_inc(work_filled[b], 1)

            def product3(o, lhs, rhs, start=True, stop=True):
                pe.matmul(o, lhs[0], rhs[0], start=start, stop=False)
                pe.matmul(o, lhs[0], rhs[1], start=False, stop=False)
                return pe.matmul(o, lhs[1], rhs[0], start=False, stop=stop)

            def turn_x(s):
                pe.wait_ge(x_loaded, 16 * (s + 1))
                b = fill_work(s, "xT")
                transposes(b, [x_in[:, t, :] for t in range(BLOCK_TILES)])

            def drained(s, kind, i=0):
                b, n = work(s, kind, i)
                pe.wait_ge(work_drained[b], n)

            def project_qk(s, i):
                for w, kind in enumerate(("q", "k")):
                    if isinstance(s, int) and i == 0:
                        pe.wait_ge(wproj_split, w + 2)
                    b = fill_work(s, kind, i)
                    if i == 0:
                        drained(s, "xT")
                    cols = slice(i * P, (i + 1) * P)
                    product3(ps_work[:, b, :], (w_hi[w][:, cols], w_lo[w][:, cols]),
                             (xT_hi[:], xT_lo[:])).then_inc(work_filled[b], 1)

            def project_v(s, u):
                if isinstance(s, int) and s == 0 and u == 0:
                    pe.wait_ge(wproj_split, 4)
                    pe.wait_ge(consts_ready, 2)
                b = fill_work(s, "v", u)
                t, half = u % 4, u // 4
                toks, cols = slice(t * P, (t + 1) * P), slice(half * 512, (half + 1) * 512)
                pe.matmul(ps_work[:, b, :], ones_rows[:], bv_parts[:, cols], start=True, stop=False)
                product3(ps_work[:, b, :], (xT_hi[:, toks], xT_lo[:, toks]), (w_hi[2][:, cols], w_lo[2][:, cols]),
                         start=False).then_inc(work_filled[b], 1)

            def scores(g, par, s, i):
                if isinstance(s, str):
                    for kind in "qk":
                        b, n = work(BLOCKS - 1, kind, 7)
                        pe.wait_ge(work_drained[b], n)
                elif i:
                    drained(s, "q", i - 1)
                    drained(s, "k", i - 1)
                else:
                    drained_before(s)
                wait(pe, exp_done, 2 * g)
                def second_tiles(hh):
                    rows = slice(hh * DH, (hh + 1) * DH)
                    for bb in range(2):
                        o, at = bb * S + P, hh * S + bb * P
                        last = pe.matmul(ps_scores[:, 2, at:at + P], kT[rows, par, o:o + P], qT[rows, par, o:o + P],
                                         start=True, stop=True)
                    return last

                second_tiles(0).then_inc(head_scored, 1)
                for bb in range(2):
                    o = bb * S
                    for hh in range(2):
                        rows = slice(hh * DH, (hh + 1) * DH)
                        pe.matmul(ps_scores[:, hh, o:o + S], kT[rows, par, o:o + P], qT[rows, par, o:o + S],
                                  start=True, stop=True)
                pe.wait_ge(head_scored, g + 1)
                second_tiles(1).then_inc(scores_ready, 1)

            def drained_before(s):
                b, n = last_keys(s)
                pe.wait_ge(work_drained[b], n)

            def contexts(g, par, pair, split=None):
                pe.wait_ge(probs_ready, 2 * (g + 1))
                wait(pe, ctx_normed, g)
                for bb in range(2):
                    if split is not None:
                        pe.wait_ge(v_split, split + 2 * (bb + 1))
                    for hh in range(2):
                        h = 2 * pair + hh
                        first, second = hh * BLOCK + bb * S, 2 * BLOCK + hh * S + bb * P
                        for qt, kt, at in ((0, 0, first), (1, 0, first + P), (1, 1, second)):
                            cols, tok = slice(at, at + P), 2 * bb + kt
                            o = ps_ctx[:, hh, (2 * bb + qt) * DV:(2 * bb + qt + 1) * DV]
                            pe.matmul(o, p_hi[:, par, cols], v_hi[:, tok, h, :], start=(kt == 0), stop=False)
                            pe.matmul(o[:, 0:DH], p_hi[:, par, cols], v_lo[:, tok, h, :], start=False, stop=False)
                            last = pe.matmul(o, p_lo[:, par, cols], v_hi[:, tok, h, :], start=False,
                                             stop=(kt == qt))
                last.then_inc(ctx_ready, 1)

            def turn_ctx(s, i, g, par):
                pe.wait_ge(ctx_normed, g + 1)
                b = fill_work(s, "ctxT", i)
                transposes(b, [ctxn[:, par, t].rearrange("p h d -> p (h d)") for t in range(BLOCK_TILES)])

            def project_out(s, chunks=range(C)):
                b = fill_work(s, "proj") if chunks[0] == 0 else work(s, "proj")[0]
                for c in chunks:
                    if c >= C - 3 and isinstance(s, str):
                        drained(s, "ctxT", c - (C - 3))
                    if c == 0 and not isinstance(s, str):
                        drained(s, "ctxT", 2)
                    cols = slice(c * P, (c + 1) * P)
                    last = product3(ps_work[:, b, :], (w_hi[3][:, cols], w_lo[3][:, cols]),
                                    (cT_hi[:, c, :], cT_lo[:, c, :]), start=(c == 0), stop=(c == C - 1))
                if c == C - 1:
                    last.then_inc(work_filled[b], 1)

            def turn_attn(s):
                drained(s, "proj")
                b = fill_work(s, "attn")
                transposes(b, [aT[:, t * P:(t + 1) * P] for t in range(BLOCK_TILES)])

            def turn_x1(s, blk):
                pe.wait_ge(x1_ready, blk + 1)
                b = fill_work(s, "x1T")
                transposes(b, [pay[:, t, 0:D] for t in range(BLOCK_TILES)])

            def affinities(s):
                drained(s, "x1T")
                b = fill_work(s, "aff")
                for t in range(BLOCK_TILES):
                    last = pe.matmul(ps_work[:, b, t * E:(t + 1) * E], x1T[:, t * P:(t + 1) * P], cenT[:],
                                     start=True, stop=True)
                last.then_inc(work_filled[b], 1)

            def ranks(s, blk):
                pe.wait_ge(chosen_ready, blk + 1)
                pe.wait_ge(seen_ready, blk + 1)
                b = fill_work(s, "rank")
                o = ps_work[:, b, 0:BLOCK_TILES * E]
                pe.matmul(o, before[:], chosen[:].rearrange("p t e -> p (t e)"), start=True, stop=False)
                pe.matmul(o, ones[:], seen[:].unsqueeze(1).broadcast_to([P, BLOCK_TILES, E]), start=False, stop=False)
                for t in range(BLOCK_TILES - 1):
                    later = BLOCK_TILES - 1 - t
                    last = pe.matmul(o[:, (t + 1) * E:], ones[:], chosen[:, t:t + 1, :].broadcast_to([P, later, E]),
                                     start=False, stop=(later == 1))
                last.then_inc(work_filled[b], 1)

            def body(s, first=False):
                for i in range(8):
                    if i or not first:
                        scores(8 * s - 1 + i, (i + 1) % 2, s, i)
                    if i == 0:
                        turn_x(s)
                        if not first:
                            contexts(8 * s - 2, 0, C - 2)
                    if i == 6 and not first:
                        turn_x1(s, s - 1)
                    project_qk(s, i)
                    if i == 0 and first:
                        pe.wait_ge(small_loaded, 16 * N_SMALL)
                        pe.transpose(ps_ctx[:, 1, 0:P], small_rows[:], ident[:]).then_inc(small_turned, 1)
                    if i >= 2 or (i and not first):
                        if i == 2 and first:
                            pe.wait_ge(small_ready, 2)
                        contexts(8 * s - 2 + i, i % 2, (i - 2) % 8, {2: 8 * s, 6: 8 * s + 4}.get(i))
                    if i == 3 and not first:
                        project_out(s)
                    if i >= 3 or not first:
                        turn_ctx(s, i, 8 * s - 3 + i, (i + 1) % 2)
                    if i < 2:
                        project_v(s, 2 * i)
                        project_v(s, 2 * i + 1)
                    if 2 <= i <= 5:
                        project_v(s, i + 2)
                    if not first:
                        if i == 4:
                            turn_attn(s)
                        if i == 6:
                            affinities(s)
                        if i == 7:
                            ranks(s, s - 1)

            pe.wait_ge(ident_ready, 1)
            pe.wait_ge(qk_bias_loaded, 32)
            pe.transpose(ps_ctx[:, 0, 0:2 * C], small_rows[0:2 * C, :], ident[0:2 * C, 0:2 * C]).then_inc(small_turned, 1)
            body(0, True)
            pe.wait_ge(wproj_split, 5)
            with pe.Fori(1, BLOCKS) as s:
                body(s)

            def turn_weights(n):
                pe.wait_ge(exp_done, 16 * BLOCKS)
                if n >= 3:
                    pe.wait_ge(turn_drained, n - 2)
                for k in range(FK):
                    src = w1n[:, n * FK + k, :] if n < E else w2n[:, n - E, k * P:(k + 1) * P]
                    last = pe.transpose(ps_scores[:, n % 3, k * P:(k + 1) * P], src, ident[:])
                last.then_inc(turned, 1)

            scores(8 * BLOCKS - 1, 1, "tail", 0)
            contexts(8 * BLOCKS - 2, 0, C - 2)
            turn_ctx("tail", 0, 8 * BLOCKS - 3, 1)
            project_out("tail", range(2))
            turn_ctx("tail", 1, 8 * BLOCKS - 2, 0)
            project_out("tail", range(2, C - 2))
            contexts(8 * BLOCKS - 1, 1, C - 1)
            project_out("tail", range(C - 2, C - 1))
            pe.wait_ge(wffn_loaded, 48)
            for n in range(0, 3):
                turn_weights(n)
            turn_ctx("tail", 2, 8 * BLOCKS - 1, 1)
            for n in range(3, 5):
                turn_weights(n)
            project_out("tail", range(C - 1, C))
            turn_weights(5)
            turn_attn("tail")
            for n in range(6, 12):
                turn_weights(n)
            turn_x1("tail", BLOCKS - 1)
            turn_weights(12)
            affinities("tail")
            for n in range(13, 16):
                turn_weights(n)
            ranks("tail", BLOCKS - 1)
            b = fill_work("tail", "count")
            pe.matmul(ps_work[:, b, 0:E], ones[:], seen[:], start=True, stop=False)
            for t in range(BLOCK_TILES):
                last = pe.matmul(ps_work[:, b, 0:E], ones[:], chosen[:, t, :], start=False, stop=(t == BLOCK_TILES - 1))
            last.then_inc(work_filled[b], 1)

            def turn_n(j):
                pe.wait_ge(nrm_ready, j + 1)
                if j >= 2:
                    pe.wait_ge(hin_ready, j - 1)
                pe.transpose(ps_work[:, j % 2, 0:P], nrm[:, j % 2, :], ident[:]).then_inc(nT_filled, 1)

            def up(j):
                pe.wait_ge(hin_ready, j + 1)
                if j >= 2:
                    pe.wait_ge(hT_ready, FK * (j - 1))
                for k in range(FK):
                    last = pe.matmul(ps_scores[:, j % 2, k * P:(k + 1) * P], wst[:, j % RING, k * P:(k + 1) * P],
                                     hin[:, j % 2, :], start=True, stop=True)
                last.then_inc(h_filled, 1)

            def down(j):
                e = experts[j]
                pe.wait_ge(hT_ready, FK * (j + 1))
                if j >= 2:
                    pe.wait_ge(f_drained, j - 1)
                for k in range(FK):
                    last = pe.matmul(ps_down[j % 2], hT[:, j % 2, k * P:(k + 1) * P],
                                     w2T[:, bass.ds(e * F + k * P, D)], start=(k == 0), stop=(k == FK - 1))
                last.then_inc(f_filled, 1)

            pe.wait_ge(turn_drained, 2 * E)
            pe.wait_ge(table_ready, 1)
            experts = table_row(0, mybir.EngineType.PE, E - 1)
            for j in range(-1, TILES + 1):
                if j + 1 < TILES:
                    turn_n(j + 1)
                if 0 <= j < TILES:
                    up(j)
                if j >= 1:
                    down(j - 1)


_INS = ['L0_attn_states', 'L0_attn_Wq', 'L0_attn_bq', 'L0_attn_Wk', 'L0_attn_bk', 'L0_attn_Wv', 'L0_attn_bv',
        'L0_attn_Wo', 'L0_attn_bo', 'L0_ffn_centroids', 'L0_ffn_ln_g', 'L0_ffn_ln_b', 'L0_ffn_w1', 'L0_ffn_b1',
        'L0_ffn_w2', 'L0_ffn_b2']
_OUTS = [((8, 256, 128), 'float32')]


def kernel(**inputs):
    import numpy as _np
    import concourse.bacc as _bacc
    from concourse import mybir as _mybir
    from concourse.bass_utils import run_bass_kernel_spmd as _run

    nc = _bacc.Bacc("TRN2", target_bir_lowering=False, num_devices=1)
    arrays, args = {}, []
    for name in _INS:
        a = _np.ascontiguousarray(inputs[name])
        arrays[f"in_{name}_dram"] = a
        args.append(nc.dram_tensor(f"in_{name}_dram", a.shape, _mybir.dt.from_np(a.dtype), kind="ExternalInput").ap())
    for i, (shape, dtype) in enumerate(_OUTS):
        dt = _mybir.dt.from_np(_np.dtype(dtype))
        args.append(nc.dram_tensor(f"out_{i}_dram", shape, dt, kind="ExternalOutput").ap())
    attention_moe(nc, *args)
    r = _run(nc, [arrays], core_ids=[0])
    got = tuple(r.results[0][f"out_{i}_dram"] for i in range(len(_OUTS)))
    return got[0]
```
